# Optimizing a Trainium2 kernel written in Bass

```python
import numpy as np
import jax
import jax.numpy as jnp

def _softmax(x, axis=-1):
    return jax.nn.softmax(x, axis=axis)

def _gelu(x):
    return jax.nn.gelu(x, approximate=True)

def _silu(x):
    return jax.nn.silu(x)

def _sigmoid(x):
    return jax.nn.sigmoid(x)

def _layernorm(x, axis=-1, eps=1e-05):
    m = jnp.mean(x, axis=axis, keepdims=True)
    v = jnp.var(x, axis=axis, keepdims=True)
    return (x - m) / jnp.sqrt(v + eps)

def _scatter_add(tgt, idx, src, axis=0):
    return tgt.at[idx].add(src)

def _segment_sum(src, seg, n):
    return jax.ops.segment_sum(src, seg, n)
kernel_name = 'mk_xattn_ffn_d1_seqx_r2_380688'

def setup_inputs(seed: int=0):
    np.random.seed(seed)
    _w = jnp.asarray

    def _rec_inputs():
        import jax
        import jax.numpy as jnp
        _rk = jax.random.key(seed)
        x = 7.22e-05 + 1 * jax.random.normal(jax.random.fold_in(_rk, 1), (8, 512, 1024), jnp.float32)
        _lenS = 512 - jax.random.randint(jax.random.fold_in(_rk, 7), (8,), 0, max(1, 512 // 4) + 1, jnp.int32)
        _lenS2 = 512 - jax.random.randint(jax.random.fold_in(_rk, 8), (8,), 0, max(1, 512 // 4) + 1, jnp.int32)
        _ctx_512P = jax.random.normal(jax.random.fold_in(_rk, 11), (8, 16, 256), jnp.float32)
        _ctx_512c = jax.random.dirichlet(jax.random.fold_in(_rk, 511), 0.3 * jnp.ones((16,), jnp.float32), (8, 512))
        _ctx_512t = jnp.einsum('bsk,bkd->bsd', _ctx_512c, _ctx_512P)
        _ctx_512t = _ctx_512t * jax.lax.rsqrt(jnp.mean(jnp.square(_ctx_512t)) + 1e-12) * 0.953939
        ctx_512 = -0.000514642 + 1.00011 * (_ctx_512t + 0.3 * jax.random.normal(jax.random.fold_in(_rk, 611), (8, 512, 256), jnp.float32))
        return (x, ctx_512)
    x, ctx_512 = _rec_inputs()

    def _L0_xattn_setup():
        import jax, jax.numpy as jnp
        import numpy as np
        import math
        NUM_Q_HEADS = 32
        NUM_KV_HEADS = 8
        key = jax.random.key(seed)
        k1, k2, k3 = jax.random.split(key, 3)
        B, S, E = (2, 1024, 1024)
        kv_E = NUM_KV_HEADS * (E // NUM_Q_HEADS)
        q = jax.random.normal(k1, (B, S, E), dtype=jnp.float32)
        k = jax.random.normal(k2, (B, S, kv_E), dtype=jnp.float32)
        v = jax.random.normal(k3, (B, S, kv_E), dtype=jnp.float32)
        return {'q': q, 'k': k, 'v': v}
    _L0_xattn_all = _L0_xattn_setup()
    _L0_xattn_in = {k: v for k, v in _L0_xattn_all.items() if k in ()}
    del _L0_xattn_all

    def _L0_ffn_setup():
        import jax, jax.numpy as jnp
        import numpy as np
        B, T, D = (4, 512, 1024)
        N, S, H = (8, 8, 8)
        ETA = 1.0
        key = jax.random.key(seed)
        ks = jax.random.split(key, 9)
        return {'x': jax.random.normal(ks[0], (B, T, D), jnp.float32), 'select_weight': jax.random.normal(ks[1], (N, D, S), jnp.float32) / D, 'select_mean_diff': jax.random.normal(ks[2], (N, D), jnp.float32) / D, 'imp_center': jax.random.normal(ks[3], (N,), jnp.float32), 'imp_slope': jax.random.normal(ks[4], (N,), jnp.float32) * 5.0, 'lora_update': jax.random.normal(ks[5], (N, D, H), jnp.float32) * 0.02, 'lora_degen': jax.random.normal(ks[6], (N, D, H), jnp.float32) * 0.02, 'bias_w': jax.random.normal(ks[7], (N, D), jnp.float32) * 0.02, 'debias_w': jax.random.normal(ks[8], (N, D), jnp.float32) * 0.02}
    _L0_ffn_all = _L0_ffn_setup()
    _L0_ffn_in = {k: v for k, v in _L0_ffn_all.items() if k in ('select_weight', 'select_mean_diff', 'imp_center', 'imp_slope', 'lora_update', 'lora_degen', 'bias_w', 'debias_w')}
    del _L0_ffn_all
    return {'x': x, 'ctx_512': ctx_512, 'L0_ffn_select_weight': _L0_ffn_in['select_weight'], 'L0_ffn_select_mean_diff': _L0_ffn_in['select_mean_diff'], 'L0_ffn_imp_center': _L0_ffn_in['imp_center'], 'L0_ffn_imp_slope': _L0_ffn_in['imp_slope'], 'L0_ffn_lora_update': _L0_ffn_in['lora_update'], 'L0_ffn_lora_degen': _L0_ffn_in['lora_degen'], 'L0_ffn_bias_w': _L0_ffn_in['bias_w'], 'L0_ffn_debias_w': _L0_ffn_in['debias_w']}

def reference(x, ctx_512, L0_ffn_select_weight, L0_ffn_select_mean_diff, L0_ffn_imp_center, L0_ffn_imp_slope, L0_ffn_lora_update, L0_ffn_lora_degen, L0_ffn_bias_w, L0_ffn_debias_w):
    import jax
    import jax.numpy as jnp

    def _L0_xattn_ref(q, k, v):
        import jax, jax.numpy as jnp
        import numpy as np
        import math
        NUM_Q_HEADS = 32
        NUM_KV_HEADS = 8
        B, S, E = q.shape
        H, KV = (NUM_Q_HEADS, NUM_KV_HEADS)
        D = E // H
        G = H // KV
        scale = math.sqrt(D)
        qh = q.reshape(B, S, KV, G, D).transpose(0, 2, 3, 1, 4)
        kh = k.reshape(B, S, KV, D).transpose(0, 2, 1, 3)
        vh = v.reshape(B, S, KV, D).transpose(0, 2, 1, 3)
        scores = jnp.einsum('bkgsd,bktd->bkgst', qh, kh) / scale
        weights = jax.nn.softmax(scores, axis=-1)
        out = jnp.einsum('bkgst,bktd->bkgsd', weights, vh)
        return out.transpose(0, 3, 1, 2, 4).reshape(B, S, E)

    def _L0_ffn_ref(x, select_weight, select_mean_diff, imp_center, imp_slope, lora_update, lora_degen, bias_w, debias_w):
        import jax, jax.numpy as jnp
        import numpy as np
        B, T, D = (4, 512, 1024)
        N, S, H = (8, 8, 8)
        ETA = 1.0
        x_diff = x[:, None, :, :] - select_mean_diff[None, :, None, :]
        x_diff = x_diff / jnp.linalg.norm(x_diff, axis=3, keepdims=True)
        cont = jnp.einsum('nds,bntd->bnts', select_weight, x_diff) ** 2
        score = cont.sum(axis=-1)
        gate = jax.nn.sigmoid(imp_slope[None, :, None] * (score - imp_center[None, :, None]))
        sel_scale = gate.max(axis=1)[..., None]
        sel_idx = gate.argmax(axis=1)
        debias = jnp.take(debias_w, sel_idx, axis=0)
        bias = jnp.take(bias_w, sel_idx, axis=0)
        upd = jnp.take(lora_update, sel_idx, axis=0)
        dgn = jnp.take(lora_degen, sel_idx, axis=0)
        x_debias = x - debias
        mod_x = jnp.einsum('btdh,btd->bth', upd, x_debias)
        degen_up = jnp.einsum('btdh,bth->btd', dgn, mod_x)
        mod_x_bias = ETA * (bias + degen_up)
        return (1.0 - sel_scale) * x + sel_scale * mod_x_bias
    x = x + _L0_xattn_ref(_layernorm(x, axis=-1), ctx_512, ctx_512)
    x = x + _L0_ffn_ref(_layernorm(x, axis=-1), L0_ffn_select_weight, L0_ffn_select_mean_diff, L0_ffn_imp_center, L0_ffn_imp_slope, L0_ffn_lora_update, L0_ffn_lora_degen, L0_ffn_bias_w, L0_ffn_debias_w)
    return x

_drawn_inputs = setup_inputs


def setup_inputs(seed=0):
    import zlib

    import numpy as np

    out = dict(_drawn_inputs(seed))
    spreads = {}
    factors = {'L0_ffn_bias_w': 3.508, 'L0_ffn_debias_w': 64.0}
    for name, (base, spread) in spreads.items():
        noise = np.random.default_rng([zlib.crc32(name.encode()), seed]).standard_normal(out[name].shape)
        drawn = base * np.exp(spread * noise) if base else spread * noise
        out[name] = jnp.asarray(drawn.astype(out[name].dtype))
    for name, factor in factors.items():
        out[name] = (out[name] * factor).astype(out[name].dtype)
    return out
```

```python
import concourse.bass as bass
from concourse import mybir
from contextlib import ExitStack


def xattn_ffn(nc: bass.Bass, x, ctx_in, sel_w, sel_mu, imp_center, imp_slope, lora_up, lora_dn,
              bias_w, debias_w, out):
    f32, f16 = mybir.dt.float32, mybir.dt.float16
    ALU = mybir.AluOpType
    ACT = mybir.ActivationFunctionType
    AX = mybir.AxisListType

    P = 128
    B, S, E = x.shape
    CE = ctx_in.shape[2]
    D = 32
    KV = CE // D
    G = E // D // KV
    ST = S // P
    CB = CE // P
    NX, _, NS = sel_w.shape
    EC = E // P
    UNITS = B * KV
    TILES = B * ST
    EPS = 1e-5
    UP = 16.0
    EXP_SCALE = 1.0 / (UP * UP * D ** 0.5)
    SHIFT_UNIT = 4096.0
    NP3 = 3 * D
    STACK = NP3 + 2
    NE = NX * NS
    WC = 2 * NE + NX
    assert G * D == P and S == 512 and NE + NX <= P

    q_scr = nc.dram_tensor("q_split", [B, 2, KV, P, S], f16, kind="Internal").ap()
    k_scr = nc.dram_tensor("k_split", [B, 2, CB, P, S], f16, kind="Internal").ap()
    m_scr = nc.dram_tensor("row_shift", [UNITS, 2, G, S], f16, kind="Internal").ap()
    y_scr = nc.dram_tensor("attended", [B, S, E], f32, kind="Internal").ap()

    def wait(eng, sem, count):
        if not isinstance(count, int) or count > 0:
            eng.wait_ge(sem, count)

    with ExitStack() as keep:
        sem = lambda name: keep.enter_context(nc.semaphore(name))
        ident = keep.enter_context(nc.sbuf_tensor("ident", [P, P], f32))
        ones = keep.enter_context(nc.sbuf_tensor("ones", [P, P], f32))
        power = keep.enter_context(nc.sbuf_tensor("power", [P, 1], f32))
        consts_set, ident_set = sem("consts_set"), sem("ident_set")

        with ExitStack() as own:
            sb = lambda name, shape, dt: own.enter_context(nc.sbuf_tensor(name, shape, dt))
            xin = sb("xin", [P, 2, E], f32)
            cin = sb("cin", [P, 2, CE], f32)
            xn = sb("xn", [P, 2, E], f32)
            stats = sb("stats", [P, 2, 2, 6], f32)
            mv = sb("mv", [P, 2, 2], f32)
            var_eps = sb("var_eps", [P, 2], f32)
            rstd = sb("rstd", [P, 2], f32)
            q_parts = sb("q_parts", [P, 2, 2, KV, 2 * P], f16)
            k_parts = sb("k_parts", [P, 2, 2, CB, 2 * P], f16)
            q_ps = own.enter_context(nc.psum_tensor("q_ps", [P, 2, KV, P], f32))
            k_ps = own.enter_context(nc.psum_tensor("k_ps", [P, 2, 4, P], f32))

            x_in = [sem("x_in0"), sem("x_in1")]
            split_out = [sem("split_out0"), sem("split_out1")]
            stats_done, mv_done, var_ready = sem("stats_done"), sem("mv_done"), sem("var_ready")
            rstd_done, xn_done = sem("rstd_done"), sem("xn_done")
            turned, high_done, low_done = sem("turned"), sem("high_done"), sem("low_done")
            block = own.enter_context(nc.Block())

            def batches(eng, body):
                body(0)
                with eng.Fori(1, B) as b:
                    body(b)

            @block.sync
            def _(sp):
                def load(b, t):
                    n = ST * b + t
                    wait(sp, xn_done, n - 1)
                    wait(sp, turned, n - 1)
                    sp.dma_start(xin[:, t % 2, :], x[bass.ds(b, 1), t * P:(t + 1) * P, :]
                                 .rearrange("o p e -> (o p) e")).then_inc(x_in[t % 2], 16)
                    sp.dma_start(cin[:, t % 2, :], ctx_in[bass.ds(b, 1), t * P:(t + 1) * P, :]
                                 .rearrange("o p e -> (o p) e")).then_inc(x_in[t % 2], 16)

                def store(b, pair):
                    n = ST * b + 2 * pair
                    wait(sp, low_done, 2 * n + 4)
                    cols = slice(2 * pair * P, (2 * pair + 2) * P)
                    sp.dma_start(q_scr[bass.ds(b, 1), :, :, :, cols].rearrange("o l h p s -> p (o l h) s"),
                                 q_parts[:, pair].rearrange("p l h s -> p (l h) s")
                                 ).then_inc(split_out[pair], 16)
                    sp.dma_start(k_scr[bass.ds(b, 1), :, :, :, cols].rearrange("o l h p s -> p (o l h) s"),
                                 k_parts[:, pair].rearrange("p l h s -> p (l h) s")
                                 ).then_inc(split_out[pair], 16)

                def body(b):
                    for t in range(ST):
                        load(b, t)
                        if t == 1 and (not isinstance(b, int) or b > 0):
                            store(b - 1, 1)
                        if t == 3:
                            store(b, 0)

                batches(sp, body)
                store(B - 1, 1)
                for pair in range(2):
                    sp.wait_ge(split_out[pair], 32 * B)

            @block.gpsimd
            def _(pool):
                pool.memset(ident[:], 0.0).then_inc(ident_set, 1)
                pool.memset(ones[:], 1.0).then_inc(consts_set, 1)
                pool.memset(power[:], -0.5).then_inc(consts_set, 1)
                pool.wait_ge(ident_set, 1)
                pool.affine_select(out=ident[:], in_=ident[:], compare_op=ALU.not_equal, fill=1.0,
                                   base=0, pattern=[[-1, P]], channel_multiplier=1
                                   ).then_inc(consts_set, 1)
                pool.wait_ge(consts_set, 3)

                def body(b):
                    for t in range(ST):
                        n, k = ST * b + t, t % 2
                        wait(pool, var_ready, n + 1)
                        wait(pool, xn_done, n - 1)
                        pool.tensor_tensor(rstd[:, k:k + 1], var_eps[:, k:k + 1], power[:], ALU.pow
                                           ).then_inc(rstd_done, 1)

                batches(pool, body)

            @block.vector
            def _(dve):
                def low(out, ps, high, n, which):
                    wait(dve, high_done, 2 * n + 1 + which)
                    dve.scalar_tensor_tensor(out=out, in0=ps, scalar=UP, in1=high, op0=ALU.mult,
                                             op1=ALU.subtract).then_inc(low_done, 1)

                def low_q(n, t):
                    k, pair, cols = t % 2, t // 2 % 2, slice(t % 2 * P, (t % 2 + 1) * P)
                    low(q_parts[:, pair, 1, :, cols], q_ps[:, k], q_parts[:, pair, 0, :, cols], n, 0)

                def low_k(n, t):
                    k, pair, cols = t % 2, t // 2 % 2, slice(t % 2 * P, (t % 2 + 1) * P)
                    low(k_parts[:, pair, 1, :, cols], k_ps[:, k, 0:CB], k_parts[:, pair, 0, :, cols], n, 1)

                def body(b):
                    for t in range(ST):
                        n, k = ST * b + t, t % 2
                        before = not isinstance(n, int) or n > 0
                        dve.wait_ge(x_in[k], 32 * (2 * b + t // 2 + 1))
                        dve.bn_stats(stats[:, k, 0, :], xin[:, k, 0:512])
                        dve.bn_stats(stats[:, k, 1, :], xin[:, k, 512:1024]).then_inc(stats_done, 1)
                        dve.wait_ge(stats_done, n + 1)
                        if before:
                            low_q(n - 1, t + 3)
                        dve.bn_aggr(mv[:, k, :], stats[:, k]).then_inc(mv_done, 1)
                        dve.wait_ge(mv_done, n + 1)
                        dve.tensor_scalar_add(var_eps[:, k:k + 1], mv[:, k, 1:2], EPS
                                              ).then_inc(var_ready, 1)
                        if before:
                            low_k(n - 1, t + 3)
                        dve.wait_ge(rstd_done, n + 1)
                        wait(dve, turned, n - 1)
                        dve.tensor_scalar(xn[:, k, :], xin[:, k, :], mv[:, k, 0:1], rstd[:, k:k + 1],
                                          ALU.subtract, ALU.mult).then_inc(xn_done, 1)

                batches(dve, body)
                low_q(TILES - 1, ST - 1)
                low_k(TILES - 1, ST - 1)

            @block.tensor
            def _(pe):
                pe.wait_ge(consts_set, 3)

                def body(b):
                    for t in range(ST):
                        n, k = ST * b + t, t % 2
                        pe.wait_ge(xn_done, n + 1)
                        wait(pe, low_done, 2 * n - 2)
                        for h in range(KV):
                            pe.transpose(q_ps[:, k, h, :], xn[:, k, h * P:(h + 1) * P], ident[:])
                        for c in range(CB):
                            last = pe.transpose(k_ps[:, k, c, :], cin[:, k, c * P:(c + 1) * P], ident[:])
                        last.then_inc(turned, 1)

                batches(pe, body)

            @block.scalar
            def _(act):
                def body(b):
                    for t in range(ST):
                        n, k, pair, half = ST * b + t, t % 2, t // 2, t % 2
                        cols = slice(half * P, (half + 1) * P)
                        act.wait_ge(turned, n + 1)
                        if half == 0:
                            wait(act, split_out[pair], 32 * b)
                        act.activation(q_parts[:, pair, 0, :, cols], q_ps[:, k], ACT.Copy, scale=UP
                                       ).then_inc(high_done, 1)
                        act.activation(k_parts[:, pair, 0, :, cols], k_ps[:, k, 0:CB], ACT.Copy, scale=UP
                                       ).then_inc(high_done, 1)

                batches(act, body)

        with ExitStack() as own2:
            sb2 = lambda name, shape, dt: own2.enter_context(nc.sbuf_tensor(name, shape, dt))
            q_stack = sb2("q_stack", [STACK, 2, G, S], f16)
            k_stack = sb2("k_stack", [STACK, 2, S], f16)
            stacks_set = sem("stacks_set")

            def load_stack(sp, b, h, k, arrived):
                of_q = q_scr[bass.ds(b, 1), :, bass.ds(h, 1), :, :].rearrange(
                    "o l c (g d) s -> d (o c l) g s", d=D)
                for row, part in enumerate((0, 0, 1)):
                    sp.dma_start(q_stack[row * D:(row + 1) * D, k], of_q[:, part]).then_inc(arrived, 16)
                of_k = k_scr[bass.ds(b, 1), :, bass.ds(h // (P // D), 1), bass.ds(h % (P // D) * D, D), :]
                of_k = of_k.rearrange("o l c d s -> d (o c l) s")
                for row, part in enumerate((0, 1, 0)):
                    sp.dma_start(k_stack[row * D:(row + 1) * D, k], of_k[:, part]).then_inc(arrived, 16)

            def pairs(eng, body):
                for k in range(2):
                    body(k, k, 0, k)
                with eng.Fori(1, UNITS // 2) as j:
                    for k in range(2):
                        body(2 * j + k, k, j // (KV // 2), j % (KV // 2) * 2 + k)

            with ExitStack() as own:
                sb = lambda name, shape, dt: own.enter_context(nc.sbuf_tensor(name, shape, dt))
                row_max = sb("row_max", [P, 2, G * ST], f32)
                shift = sb("shift", [G * ST, 2, 2, P], f16)
                NCH = G * ST // 2
                s_ps = own.enter_context(nc.psum_tensor("s_ps", [P, 2, 2, S], f32))
                m_ps = own.enter_context(nc.psum_tensor("m_ps", [G * ST, 2, 512], f32))
                m_in = [sem("m_in0"), sem("m_in1")]
                m_out = [sem("m_out0"), sem("m_out1")]
                scored, reduced, max_turned = sem("scored"), sem("reduced"), sem("max_turned")
                shift_high, shift_low = sem("shift_high"), sem("shift_low")
                block = own.enter_context(nc.Block())

                @block.gpsimd
                def _(pool):
                    pool.memset(k_stack[NP3:STACK], SHIFT_UNIT).then_inc(stacks_set, 1)

                @block.sync
                def _(sp):
                    def store(u, k):
                        wait(sp, shift_low, u + 1)
                        sp.dma_start(m_scr[bass.ds(u, 1)].rearrange("o l g (t s) -> (g t) (o l) s", t=ST),
                                     shift[:, k]).then_inc(m_out[k], 16)

                    def body(u, k, b, h):
                        wait(sp, scored, NCH * (u - 1))
                        load_stack(sp, b, h, k, m_in[k])
                        if not isinstance(u, int) or u >= 2:
                            store(u - 2, k)

                    pairs(sp, body)
                    for k in range(2):
                        store(UNITS - 2 + k, k)
                    for k in range(2):
                        sp.wait_ge(m_out[k], 16 * (UNITS // 2))

                @block.tensor
                def _(pe):
                    def turn_max(u, k):
                        wait(pe, reduced, NCH * (u + 1))
                        wait(pe, shift_low, u - 1)
                        pe.transpose(m_ps[:, k, 0:P], row_max[:, k, :], ident[:]).then_inc(max_turned, 1)

                    def body(u, k, b, h):
                        wait(pe, m_in[k], 96 * ((u - k) // 2 + 1))
                        for c in range(NCH):
                            wait(pe, reduced, NCH * u + c - 1)
                            for i in range(2):
                                g, t = (2 * c + i) // ST, (2 * c + i) % ST
                                last = pe.matmul(s_ps[:, c % 2, i, :],
                                                 q_stack[0:NP3, k, g, t * P:(t + 1) * P],
                                                 k_stack[0:NP3, k, :], start=True, stop=True)
                            last.then_inc(scored, 1)
                            if c == 1 and (not isinstance(u, int) or u >= 1):
                                turn_max(u - 1, 1 - k)

                    pairs(pe, body)
                    turn_max(UNITS - 1, 1)

                @block.vector
                def _(dve):
                    def low(u, k):
                        wait(dve, shift_high, u + 1)
                        dve.scalar_tensor_tensor(out=shift[:, k, 1, :], in0=m_ps[:, k, 0:P],
                                                 scalar=-1.0 / SHIFT_UNIT, in1=shift[:, k, 0, :],
                                                 op0=ALU.mult, op1=ALU.subtract).then_inc(shift_low, 1)

                    def body(u, k, b, h):
                        wait(dve, max_turned, u - 1)
                        for c in range(NCH):
                            wait(dve, scored, NCH * u + c + 1)
                            dve.reduce_max(row_max[:, k, 2 * c:2 * c + 2], s_ps[:, c % 2], AX.X
                                           ).then_inc(reduced, 1)
                            if c == 4 and (not isinstance(u, int) or u >= 1):
                                low(u - 1, 1 - k)

                    pairs(dve, body)
                    low(UNITS - 1, 1)

                @block.scalar
                def _(act):
                    def body(u, k, b, h):
                        wait(act, max_turned, u + 1)
                        wait(act, m_out[k], 16 * ((u - k) // 2))
                        act.activation(shift[:, k, 0, :], m_ps[:, k, 0:P], ACT.Copy,
                                       scale=-1.0 / SHIFT_UNIT).then_inc(shift_high, 1)

                    pairs(act, body)

            with ExitStack() as own:
                sb = lambda name, shape, dt: own.enter_context(nc.sbuf_tensor(name, shape, dt))
                v_in = sb("v_in", [P, 2, ST, D], f32)
                x_res = sb("x_res", [P, 2, ST, P], f32)
                x_att = sb("x_att", [P, 2, ST, P], f32)
                probs = sb("probs", [P, 2, ST, G, S], f32)
                sum_front = sb("sum_front", [P, G, S], f32)
                sum_back = sb("sum_back", [P, G, S], f32)
                sum_all = sb("sum_all", [P, G, S], f32)
                o_raw = sb("o_raw", [P, 2, S], f32)
                den_t = sb("den_t", [P, S], f32)
                inv_t = sb("inv_t", [P, S // D], f32)
                inv = sb("inv", [P, S], f32)
                o_norm = sb("o_norm", [P, S], f32)
                NCH = ST * G // 2
                RING = 3
                s_ps = own.enter_context(nc.psum_tensor("st_ps", [P, RING, 2, S], f32))
                o_ps = own.enter_context(nc.psum_tensor("o_ps", [P, S], f32))
                dt_ps = own.enter_context(nc.psum_tensor("dt_ps", [P, S], f32))
                a_in = [sem("a_in0"), sem("a_in1")]
                v_sem = [sem("v_in0"), sem("v_in1")]
                res_in = [sem("res_in0"), sem("res_in1")]
                a_out = [sem("a_out0"), sem("a_out1")]
                scored, exped, pv_done = sem("scored_t"), sem("exped"), sem("pv_done")
                front_done, back_done, all_done = sem("front_done"), sem("back_done"), sem("all_done")
                den_done, o_copied, o_turned = sem("den_done"), sem("o_copied"), sem("o_turned")
                den_turned, inv_made, inv_spread = sem("den_turned"), sem("inv_made"), sem("inv_spread")
                o_normed, res_added = sem("o_normed"), sem("res_added")
                block = own.enter_context(nc.Block())

                CYCLE = 6

                def units(eng, body, start=0, lag=0):
                    for u in range(CYCLE):
                        body(u, u, u // KV, u % KV)
                    with eng.Fori(1, UNITS // CYCLE) as j:
                        for k in range(CYCLE):
                            u = CYCLE * j + k
                            body(u, k, u // KV, u % KV)
                    for u in range(UNITS // CYCLE * CYCLE, UNITS):
                        body(u, u % CYCLE, u // KV, u % KV)

                at_least = lambda u, least: not isinstance(u, int) or u >= least

                @block.sync
                def _(sp):
                    def store(u, k, b, h):
                        wait(sp, res_added, u + 1)
                        sp.dma_start(y_scr[bass.ds(b, 1), :, bass.ds(h * P, P)]
                                     .rearrange("o (t p) e -> p (o t) e", p=P), x_att[:, k % 2]
                                     ).then_inc(a_out[k % 2], 16)

                    def load_res(u, k, b, h):
                        wait(sp, res_added, u - 1)
                        sp.dma_start(x_res[:, k % 2], x[bass.ds(b, 1), :, bass.ds(h * P, P)]
                                     .rearrange("o (t p) e -> p (o t) e", p=P)).then_inc(res_in[k % 2], 16)

                    def body(u, k, b, h):
                        s = k % 2
                        wait(sp, scored, NCH * (u - 1))
                        load_stack(sp, b, h, s, a_in[s])
                        sp.dma_start(q_stack[NP3:STACK, s], m_scr[bass.ds(u, 1)]
                                     .rearrange("o l g s -> (o l) g s")).then_inc(a_in[s], 16)
                        wait(sp, pv_done, ST * (u - 1))
                        sp.dma_start(v_in[:, s], ctx_in[bass.ds(b, 1), :, bass.ds(h * D, D)]
                                     .rearrange("o (t p) d -> p (o t) d", p=P)).then_inc(v_sem[s], 16)
                        if at_least(u, 1):
                            load_res(u - 1, k + 1, (u - 1) // KV, (u - 1) % KV)
                        if at_least(u, 3):
                            store(u - 3, k + 3, (u - 3) // KV, (u - 3) % KV)

                    units(sp, body)
                    load_res(UNITS - 1, UNITS - 1, B - 1, KV - 1)
                    for u in range(UNITS - 3, UNITS):
                        store(u, u, u // KV, u % KV)
                    for s in range(2):
                        sp.wait_ge(a_out[s], 16 * (UNITS // 2))

                @block.tensor
                def _(pe):
                    pe.wait_ge(stacks_set, 1)

                    def score(u, k, c):
                        s, t, slot = k % 2, c // 2, (NCH * k + c) % RING
                        wait(pe, exped, NCH * u + c - RING + 1)
                        for i in range(2):
                            last = pe.matmul(s_ps[:, slot, i, :], k_stack[:, s, t * P:(t + 1) * P],
                                             q_stack[:, s, 2 * (c % 2) + i, :], start=True, stop=True)
                        last.then_inc(scored, 1)

                    def weigh(u, k, t):
                        s = k % 2
                        wait(pe, exped, NCH * u + 2 * t + 2)
                        if t == 0:
                            wait(pe, v_sem[s], 16 * ((u - s) // 2 + 1))
                            wait(pe, o_copied, u)
                        for g in range(G):
                            last = pe.matmul(o_ps[g * D:(g + 1) * D, :], v_in[:, s, t, :],
                                             probs[:, s, t, g, :], start=(t == 0), stop=(t == ST - 1))
                        last.then_inc(pv_done, 1)

                    def denominators(u):
                        wait(pe, all_done, u + 1)
                        wait(pe, res_added, u)
                        for g in range(G):
                            last = pe.matmul(dt_ps[g * D:(g + 1) * D, :], ones[:, 0:D],
                                             sum_all[:, g, :], start=True, stop=True)
                        last.then_inc(den_done, 1)

                    def turn_out(u):
                        wait(pe, o_normed, u + 1)
                        for t in range(ST):
                            last = pe.transpose(dt_ps[:, t * P:(t + 1) * P], o_norm[:, t * P:(t + 1) * P],
                                                ident[:])
                        last.then_inc(o_turned, 1)

                    def arrived(u, k):
                        wait(pe, a_in[k % 2], 112 * ((u - k % 2) // 2 + 1))

                    arrived(0, 0)
                    for c in range(NCH):
                        score(0, 0, c) if c < RING else None
                    rest = list(range(RING, NCH))

                    def body(u, k, b, h):
                        more = not isinstance(u, int) or u < UNITS - 1
                        if more:
                            arrived(u + 1, k + 1)
                        for t in range(ST):
                            if more:
                                score(u + 1, k + 1, 2 * t)
                                score(u + 1, k + 1, 2 * t + 1)
                            if t == 0 and at_least(u, 1):
                                denominators(u - 1)
                            if t == ST - 1 and at_least(u, 1):
                                turn_out(u - 1)
                            weigh(u, k, t)

                    for c in rest:
                        score(0, 0, c)
                    units(pe, body)
                    denominators(UNITS - 1)
                    turn_out(UNITS - 1)

                @block.scalar
                def _(act):
                    def exps(u, k):
                        s = k % 2
                        for c in range(NCH):
                            t = c // 2
                            if c % 2 == 0:
                                wait(act, pv_done, ST * (u - 2) + t + 1)
                                wait(act, front_done if t < ST // 2 else back_done, u - 1)
                            wait(act, scored, NCH * u + c + 1)
                            act.activation(probs[:, s, t, 2 * (c % 2):2 * (c % 2) + 2, :],
                                           s_ps[:, (NCH * k + c) % RING], ACT.Exp, scale=EXP_SCALE
                                           ).then_inc(exped, 1)

                    def copy_out(u, k):
                        wait(act, pv_done, ST * (u + 1))
                        wait(act, o_normed, u - 1)
                        act.activation(o_raw[:, k % 2, :], o_ps[:], ACT.Copy).then_inc(o_copied, 1)

                    def body(u, k, b, h):
                        if at_least(u, 2):
                            copy_out(u - 2, k)
                        exps(u, k)

                    units(act, body)
                    for u in range(UNITS - 2, UNITS):
                        copy_out(u, u)

                @block.gpsimd
                def _(pool):
                    def body(u, k, b, h):
                        wait(pool, exped, NCH * (u + 1))
                        wait(pool, all_done, u)
                        pool.tensor_tensor(sum_back[:], probs[:, k % 2, 2], probs[:, k % 2, 3], ALU.add
                                           ).then_inc(back_done, 1)

                    units(pool, body)

                @block.vector
                def _(dve):
                    def sum_up(u, k):
                        wait(dve, exped, NCH * u + NCH // 2)
                        wait(dve, all_done, u)
                        dve.tensor_tensor(sum_front[:], probs[:, k % 2, 0], probs[:, k % 2, 1], ALU.add
                                          ).then_inc(front_done, 1)

                    def normalise(u, k):
                        wait(dve, den_done, u + 1)
                        dve.transpose(den_t[:], dt_ps[:]).then_inc(den_turned, 1)
                        wait(dve, den_turned, u + 1)
                        dve.reciprocal(inv_t[:], den_t[:, 0:S:D]).then_inc(inv_made, 1)
                        wait(dve, inv_made, u + 1)
                        dve.transpose(inv[:].rearrange("p (a b) -> p a b", b=D),
                                      inv_t[:].unsqueeze(2).to_broadcast([P, S // D, D])
                                      ).then_inc(inv_spread, 1)
                        wait(dve, inv_spread, u + 1)
                        wait(dve, o_copied, u + 1)
                        wait(dve, o_turned, u)
                        dve.tensor_tensor(o_norm[:], o_raw[:, k % 2, :], inv[:], ALU.mult
                                          ).then_inc(o_normed, 1)

                    def total(u):
                        wait(dve, back_done, u + 1)
                        wait(dve, front_done, u + 1)
                        wait(dve, den_done, u)
                        dve.tensor_tensor(sum_all[:], sum_front[:], sum_back[:], ALU.add
                                          ).then_inc(all_done, 1)

                    def add_res(u, k):
                        s = k % 2
                        wait(dve, o_turned, u + 1)
                        wait(dve, res_in[s], 16 * ((u - s) // 2 + 1))
                        wait(dve, a_out[s], 16 * ((u - s) // 2))
                        dve.tensor_tensor(x_att[:, s].rearrange("p t e -> p (t e)"),
                                          x_res[:, s].rearrange("p t e -> p (t e)"), dt_ps[:], ALU.add
                                          ).then_inc(res_added, 1)

                    def body(u, k, b, h):
                        sum_up(u, k)
                        if at_least(u, 1):
                            normalise(u - 1, k + 1)
                        total(u)
                        if at_least(u, 1):
                            add_res(u - 1, k + 1)

                    units(dve, body)
                    normalise(UNITS - 1, UNITS - 1)
                    add_res(UNITS - 1, UNITS - 1)

        with ExitStack() as own:
            sb = lambda name, shape, dt: own.enter_context(nc.sbuf_tensor(name, shape, dt))
            SLOTS = 3
            sel_sb = sb("sel_sb", [P, NX, EC, NS], f32)
            upd_sb = sb("upd_sb", [P, NX, EC, NS], f32)
            deg_sb = sb("deg_sb", [P, NX, EC, NS], f32)
            deg_cols = sb("deg_cols", [P, EC, NE], f32)
            mu_sb = sb("mu_sb", [P, NX, EC], f32)
            deb_sb = sb("deb_sb", [P, NX, EC], f32)
            w_all = sb("w_all", [P, EC, WC], f32)
            down = sb("down", [P, E], f32)
            prod = sb("prod", [P, 3, NX, NS, EC], f32)
            c_part = sb("c_part", [P, WC + 2 * NX], f32)
            cst = sb("cst", [P, WC + 2 * NX], f32)
            neg_slope = sb("neg_slope", [P, NX], f32)
            rank = sb("rank", [P, NX], f32)
            xa = sb("xa", [P, SLOTS, E], f32)
            y = sb("y", [P, SLOTS, E], f32)
            yT = sb("yT", [P, EC, P], f32)
            xy = sb("xy", [P, E], f32)
            x_out = sb("x_out", [P, SLOTS, E], f32)
            mixT = sb("mixT", [P, P], f32)
            mix = sb("mix", [P, SLOTS, P], f32)
            stats = sb("stats3", [P, 2, 6], f32)
            mv = sb("mv3", [P, SLOTS, 2], f32)
            var_eps = sb("var_eps3", [P, 1], f32)
            rstd = sb("rstd3", [P, SLOTS], f32)
            y_sq = sb("y_sq", [P, SLOTS], f32)
            diff = sb("diff", [P, 2 * NE], f32)
            sq = sb("sq", [P, NE], f32)
            small = sb("small", [P, 12, NX], f32)
            z_e = sb("z_e", [P, NX], f32)
            keep_x = sb("keep_x", [P, SLOTS], f32)
            y_ps = own.enter_context(nc.psum_tensor("y_ps", [P, EC, P], f32))
            z_ps = own.enter_context(nc.psum_tensor("z_ps", [P, 512], f32))
            mix_ps = own.enter_context(nc.psum_tensor("mix_ps", [P, 512], f32))
            r_ps = own.enter_context(nc.psum_tensor("r_ps", [P, E], f32))

            w_in, zeroed, prep, folded = sem("w_in"), sem("zeroed"), sem("prep"), sem("folded")
            down_turned, down_copied, cst_done = sem("down_turned"), sem("down_copied"), sem("cst_done")
            t_in = [sem(f"t_in{i}") for i in range(SLOTS)]
            t_out = [sem(f"t_out{i}") for i in range(SLOTS)]
            ln_chain, gate_chain, xy_done = sem("ln_chain"), sem("gate_chain"), sem("xy_done")
            var_ready, rstd_done, y_done = sem("var_ready3"), sem("rstd_done3"), sem("y_done")
            y_turned, yT_done, z_done = sem("y_turned"), sem("yT_done"), sem("z_done")
            z_read, e_ready, e_done, mix_done = sem("z_read"), sem("e_ready"), sem("e_done"), sem("mix_done")
            mix_turned, mixT_done, r_done, final = sem("mix_turned"), sem("mixT_done"), sem("r_done"), sem("final")
            block = own.enter_context(nc.Block())

            LAGS = 2

            def steps(eng, body):
                for i in range(SLOTS):
                    body(i, i)
                with eng.Fori(1, TILES // SLOTS) as j:
                    for k in range(SLOTS):
                        body(SLOTS * j + k, k)
                for i in range(TILES // SLOTS * SLOTS, TILES + LAGS):
                    body(i, i % SLOTS)

            live = lambda i: not isinstance(i, int) or 0 <= i < TILES
            x_tiles = y_scr.rearrange("b (t p) e -> (b t) p e", p=P)
            o_tiles = out.rearrange("b (t p) e -> (b t) p e", p=P)

            @block.sync
            def _(sp):
                for dst, src in ((sel_sb, sel_w), (upd_sb, lora_up), (deg_sb, lora_dn)):
                    sp.dma_start(dst[:].rearrange("p n c s -> p n (c s)"),
                                 src.rearrange("n (p c) s -> p n (c s)", c=EC)).then_inc(w_in, 16)
                sp.dma_start(mu_sb[:], sel_mu.rearrange("n (p c) -> p n c", c=EC)).then_inc(w_in, 16)
                sp.dma_start(deb_sb[:], debias_w.rearrange("n (p c) -> p n c", c=EC)).then_inc(w_in, 16)
                sp.wait_ge(zeroed, 3)
                sp.dma_start(down[NE:NE + NX, :], bias_w).then_inc(w_in, 16)
                sp.dma_start(c_part[0:1, WC:WC + NX], imp_center.rearrange("(o n) -> o n", o=1)).then_inc(w_in, 16)
                sp.dma_start(c_part[0:1, WC + NX:], imp_slope.rearrange("(o n) -> o n", o=1)).then_inc(w_in, 16)

                def body(i, k):
                    if live(i):
                        wait(sp, final, i - 2)
                        sp.dma_start(xa[:, k, :], x_tiles[bass.ds(i, 1)].rearrange("o p e -> (o p) e")
                                     ).then_inc(t_in[k], 16)
                    if live(i - 2):
                        wait(sp, final, i - 1)
                        sp.dma_start(o_tiles[bass.ds(i - 2, 1)].rearrange("o p e -> (o p) e"),
                                     x_out[:, (k + 1) % SLOTS, :]).then_inc(t_out[(k + 1) % SLOTS], 16)

                steps(sp, body)
                for k in range(SLOTS):
                    sp.wait_ge(t_out[k], 16 * len(range(k, TILES, SLOTS)))

            @block.gpsimd
            def _(pool):
                pool.memset(c_part[:], 0.0).then_inc(zeroed, 1)
                pool.memset(down[:], 0.0).then_inc(zeroed, 1)
                pool.memset(mix[:], 0.0).then_inc(zeroed, 1)
                for n in range(NX):
                    pool.memset(rank[:, n:n + 1], float(NX - n)).then_inc(zeroed, 1)

                def body(i, k):
                    if live(i):
                        wait(pool, var_ready, i + 1)
                        pool.tensor_tensor(rstd[:, k:k + 1], var_eps[:], power[:], ALU.pow
                                           ).then_inc(rstd_done, 1)

                steps(pool, body)

            @block.tensor
            def _(pe):
                pe.wait_ge(prep, 1)
                for half in range(2):
                    if half:
                        pe.wait_ge(down_copied, 1)
                    for i in range(4):
                        last = pe.transpose(mix_ps[0:NE, i * P:(i + 1) * P],
                                            deg_cols[:, 4 * half + i, :], ident[:])
                    last.then_inc(down_turned, 1)
                pe.wait_ge(prep, 5)
                pe.matmul(z_ps[:, 0:WC + 2 * NX], ones[:], c_part[:], start=True, stop=True
                          ).then_inc(folded, 1)
                pe.wait_ge(cst_done, 2)

                def body(i, k):
                    if live(i - 1):
                        wait(pe, yT_done, i)
                        wait(pe, z_read, i - 1)
                        for c in range(EC):
                            last = pe.matmul(z_ps[:, 0:WC], yT[:, c, :], w_all[:, c, :],
                                             start=(c == 0), stop=(c == EC - 1))
                        last.then_inc(z_done, 1)
                    if live(i - 2):
                        wait(pe, mix_done, i - 1)
                        pe.transpose(mix_ps[:, 0:P], mix[:, (k + 1) % SLOTS, :], ident[:]
                                     ).then_inc(mix_turned, 1)
                        wait(pe, mixT_done, i - 1)
                        wait(pe, final, i - 2)
                        for half in range(2):
                            last = pe.matmul(r_ps[:, half * 512:(half + 1) * 512], mixT[:],
                                             down[:, half * 512:(half + 1) * 512], start=True, stop=True)
                        last.then_inc(r_done, 1)
                    if live(i):
                        wait(pe, y_done, i + 1)
                        wait(pe, yT_done, i)
                        for c in range(EC):
                            last = pe.transpose(y_ps[:, c, :], y[:, k, c:E:EC], ident[:])
                        last.then_inc(y_turned, 1)

                steps(pe, body)

            @block.scalar
            def _(act):
                act.wait_ge(zeroed, 2)
                for half in range(2):
                    act.wait_ge(down_turned, half + 1)
                    act.activation(down[0:NE, :].rearrange("m (p c) -> m c p", c=EC)[:, 4 * half:4 * half + 4, :],
                                   mix_ps[0:NE, :].rearrange("m (c p) -> m c p", c=4), ACT.Copy
                                   ).then_inc(down_copied, 1)
                act.wait_ge(folded, 1)
                act.activation(cst[:], z_ps[:, 0:WC + 2 * NX], ACT.Copy).then_inc(cst_done, 1)
                act.wait_ge(cst_done, 1)
                act.activation(neg_slope[:], cst[:, WC + NX:], ACT.Copy, scale=-1.0).then_inc(cst_done, 1)

                def body(i, k):
                    if live(i - 2):
                        wait(act, mix_turned, i - 1)
                        wait(act, r_done, i - 2)
                        act.activation(mixT[:], mix_ps[:, 0:P], ACT.Copy).then_inc(mixT_done, 1)
                    if live(i - 1):
                        wait(act, e_ready, i)
                        act.activation(z_e[:], small[:, 5, :], ACT.Exp).then_inc(e_done, 1)
                    if live(i):
                        wait(act, y_turned, i + 1)
                        wait(act, z_done, i)
                        act.activation(yT[:], y_ps[:], ACT.Copy).then_inc(yT_done, 1)

                steps(act, body)

            @block.vector
            def _(dve):
                dve.wait_ge(w_in, 128)
                dve.wait_ge(zeroed, 3 + NX)
                for n, w in enumerate((sel_sb, upd_sb)):
                    dve.tensor_copy(w_all[:, :, n * NE:(n + 1) * NE].rearrange("p c (n s) -> p c n s", n=NX),
                                    w[:].rearrange("p n c s -> p c n s"))
                dve.tensor_copy(deg_cols[:].rearrange("p c (n s) -> p c n s", n=NX),
                                deg_sb[:].rearrange("p n c s -> p c n s"))
                dve.tensor_copy(w_all[:, :, 2 * NE:], mu_sb[:].rearrange("p n c -> p c n")).then_inc(prep, 1)
                for n, (w, m) in enumerate(((sel_sb, mu_sb), (upd_sb, deb_sb))):
                    dve.tensor_tensor(prod[:, n], w[:].rearrange("p n c s -> p n s c"),
                                      m[:].unsqueeze(2).to_broadcast([P, NX, NS, EC]), ALU.mult)
                dve.tensor_tensor(prod[:, 2, :, 0, :], mu_sb[:], mu_sb[:], ALU.mult).then_inc(prep, 1)
                dve.wait_ge(prep, 2)
                for n in range(2):
                    dve.reduce_sum(c_part[:, n * NE:(n + 1) * NE],
                                   prod[:, n].rearrange("p n s c -> p (n s) c"), AX.X).then_inc(prep, 1)
                dve.reduce_sum(c_part[:, 2 * NE:WC], prod[:, 2, :, 0, :], AX.X).then_inc(prep, 1)
                dve.wait_ge(cst_done, 2)

                LN, GATE = 4, 15
                row = lambda j: small[:, j, :]

                def normalise(i, k):
                    wait(dve, t_in[k], 16 * ((i - k) // SLOTS + 1))
                    dve.bn_stats(stats[:, 0, :], xa[:, k, 0:512])
                    dve.bn_stats(stats[:, 1, :], xa[:, k, 512:1024]).then_inc(ln_chain, 1)
                    dve.wait_ge(ln_chain, LN * i + 1)
                    if live(i - 2):
                        skip_part(i - 2, (k + 1) % SLOTS)
                    dve.bn_aggr(mv[:, k, :], stats[:]).then_inc(ln_chain, 1)
                    dve.wait_ge(ln_chain, LN * i + 2)
                    wait(dve, rstd_done, i)
                    dve.tensor_scalar_add(var_eps[:], mv[:, k, 1:2], EPS).then_inc(var_ready, 1)
                    dve.wait_ge(rstd_done, i + 1)
                    dve.tensor_scalar(y[:, k, :], xa[:, k, :], mv[:, k, 0:1], rstd[:, k:k + 1],
                                      ALU.subtract, ALU.mult).then_inc(y_done, 1)
                    dve.scalar_tensor_tensor(out=y_sq[:, k:k + 1], in0=rstd[:, k:k + 1],
                                             scalar=float(E), in1=rstd[:, k:k + 1], op0=ALU.mult,
                                             op1=ALU.mult).then_inc(ln_chain, 1)
                    dve.wait_ge(ln_chain, LN * i + 3)
                    dve.tensor_scalar(y_sq[:, k:k + 1], y_sq[:, k:k + 1], mv[:, k, 1:2], None,
                                      ALU.mult).then_inc(ln_chain, 1)

                def gate(i, k):
                    count = [0]

                    def link(ins):
                        count[0] += 1
                        ins.then_inc(gate_chain, 1)
                        dve.wait_ge(gate_chain, GATE * i + count[0])

                    wait(dve, mix_done, i)
                    wait(dve, z_done, i + 1)
                    link(dve.tensor_tensor(diff[:], z_ps[:, 0:2 * NE], cst[:, 0:2 * NE], ALU.subtract))
                    dve.scalar_tensor_tensor(out=row(0), in0=z_ps[:, 2 * NE:WC], scalar=-2.0,
                                             in1=cst[:, 2 * NE:WC], op0=ALU.mult, op1=ALU.add
                                             ).then_inc(z_read, 1)
                    link(dve.tensor_tensor(sq[:], diff[:, 0:NE], diff[:, 0:NE], ALU.mult))
                    dve.wait_ge(z_read, i + 1)
                    link(dve.tensor_scalar(row(1), row(0), y_sq[:, k:k + 1], None, ALU.add))
                    link(dve.reduce_sum(row(2), sq[:].rearrange("p (n s) -> p n s", n=NX), AX.X))
                    link(dve.reciprocal(row(3), row(1)))
                    link(dve.tensor_tensor(row(4), row(2), row(3), ALU.mult))
                    link(dve.tensor_tensor(row(6), row(4), cst[:, WC:WC + NX], ALU.subtract))
                    link(dve.tensor_tensor(row(7), row(6), neg_slope[:], ALU.mult))
                    wait(dve, e_done, i)
                    dve.tensor_scalar_min(row(5), row(7), 87.0).then_inc(e_ready, 1)
                    wait(dve, e_done, i + 1)
                    link(dve.tensor_scalar_add(row(8), z_e[:], 1.0))
                    link(dve.reciprocal(row(9), row(8)))
                    link(dve.reduce_max(row(10)[:, 0:1], row(9), AX.X))
                    link(dve.scalar_tensor_tensor(out=row(11), in0=row(9), scalar=row(10)[:, 0:1],
                                                  in1=rank[:], op0=ALU.is_ge, op1=ALU.mult))
                    link(dve.reduce_max(row(10)[:, 1:2], row(11), AX.X))
                    wait(dve, mix_turned, i - 2)
                    link(dve.tensor_scalar(mix[:, k, NE:NE + NX], row(11), row(10)[:, 1:2],
                                           row(10)[:, 0:1], ALU.is_equal, ALU.mult))
                    link(dve.tensor_scalar(keep_x[:, k:k + 1], row(10)[:, 0:1], -1.0, 1.0,
                                           ALU.mult, ALU.add))
                    dve.tensor_tensor(mix[:, k, 0:NE].rearrange("p (n s) -> p n s", n=NX),
                                      diff[:, NE:].rearrange("p (n s) -> p n s", n=NX),
                                      mix[:, k, NE:NE + NX].unsqueeze(2).to_broadcast([P, NX, NS]),
                                      ALU.mult).then_inc(mix_done, 1)
                    assert count[0] == GATE, count

                def skip_part(i, k):
                    wait(dve, final, i)
                    dve.scalar_tensor_tensor(out=xy[:], in0=y[:, k, :], scalar=keep_x[:, k:k + 1],
                                             in1=xa[:, k, :], op0=ALU.mult, op1=ALU.add
                                             ).then_inc(xy_done, 1)

                def finish(i, k):
                    wait(dve, xy_done, i + 1)
                    wait(dve, r_done, i + 1)
                    wait(dve, t_out[k], 16 * ((i - k) // SLOTS))
                    dve.tensor_tensor(x_out[:, k, :], xy[:], r_ps[:], ALU.add).then_inc(final, 1)

                def body(i, k):
                    if live(i):
                        normalise(i, k)
                    if live(i - 1):
                        gate(i - 1, (k + 2) % SLOTS)
                    if live(i - 2):
                        if not live(i):
                            skip_part(i - 2, (k + 1) % SLOTS)
                        finish(i - 2, (k + 1) % SLOTS)

                steps(dve, body)


_INS = ['x', 'ctx_512', 'L0_ffn_select_weight', 'L0_ffn_select_mean_diff', 'L0_ffn_imp_center',
        'L0_ffn_imp_slope', 'L0_ffn_lora_update', 'L0_ffn_lora_degen', 'L0_ffn_bias_w',
        'L0_ffn_debias_w']


def kernel(**inputs):
    import numpy as _np
    import concourse.bacc as _bacc
    from concourse import mybir as _mybir
    from concourse.bass_utils import run_bass_kernel_spmd as _run

    nc = _bacc.Bacc("TRN2", target_bir_lowering=False, num_devices=1)
    arrays, args = {}, []
    for name in _INS:
        a = _np.ascontiguousarray(inputs[name])
        arrays[f"in_{name}_dram"] = a
        args.append(nc.dram_tensor(f"in_{name}_dram", a.shape, _mybir.dt.from_np(a.dtype), kind="ExternalInput").ap())
    args.append(nc.dram_tensor("out_0_dram", inputs['x'].shape, _mybir.dt.float32, kind="ExternalOutput").ap())
    xattn_ffn(nc, *args)
    r = _run(nc, [arrays], core_ids=[0])
    return r.results[0]["out_0_dram"]
```

```python
import concourse.bass as bass
from concourse import mybir
from contextlib import ExitStack


def xattn_ffn(nc: bass.Bass, x, ctx_in, sel_w, sel_mu, imp_center, imp_slope, lora_up, lora_dn,
              bias_w, debias_w, out):
    f32, f16 = mybir.dt.float32, mybir.dt.float16
    ALU = mybir.AluOpType
    ACT = mybir.ActivationFunctionType
    AX = mybir.AxisListType

    P = 128
    B, S, E = x.shape
    CE = ctx_in.shape[2]
    D = 32
    KV = CE // D
    G = E // D // KV
    ST = S // P
    CB = CE // P
    NX, _, NS = sel_w.shape
    EC = E // P
    UNITS = B * KV
    TILES = B * ST
    EPS = 1e-5
    UP = 16.0
    EXP_SCALE = 1.0 / (UP * UP * D ** 0.5)
    SHIFT_UNIT = 4096.0
    NP3 = 3 * D
    STACK = NP3 + 2
    NE = NX * NS
    WC = 2 * NE + NX
    assert G * D == P and S == 512 and NE + NX <= P

    q_scr = nc.dram_tensor("q_split", [B, 2, KV, P, S], f16, kind="Internal").ap()
    k_scr = nc.dram_tensor("k_split", [B, 2, CB, P, S], f16, kind="Internal").ap()
    m_scr = nc.dram_tensor("row_shift", [UNITS, 2, G, S], f16, kind="Internal").ap()
    y_scr = nc.dram_tensor("attended", [B, S, E], f32, kind="Internal").ap()

    def wait(eng, sem, count):
        if not isinstance(count, int) or count > 0:
            eng.wait_ge(sem, count)

    with ExitStack() as keep:
        sem = lambda name: keep.enter_context(nc.semaphore(name))
        ident = keep.enter_context(nc.sbuf_tensor("ident", [P, P], f32))
        ones = keep.enter_context(nc.sbuf_tensor("ones", [P, P], f32))
        power = keep.enter_context(nc.sbuf_tensor("power", [P, 1], f32))
        consts_set, ident_set = sem("consts_set"), sem("ident_set")

        with ExitStack() as own:
            sb = lambda name, shape, dt: own.enter_context(nc.sbuf_tensor(name, shape, dt))
            xin = sb("xin", [P, 2, E], f32)
            cin = sb("cin", [P, 2, CE], f32)
            xn = sb("xn", [P, 2, E], f32)
            stats = sb("stats", [P, 2, 2, 6], f32)
            mv = sb("mv", [P, 2, 2], f32)
            var_eps = sb("var_eps", [P, 2], f32)
            rstd = sb("rstd", [P, 2], f32)
            q_parts = sb("q_parts", [P, 2, 2, KV, 2 * P], f16)
            k_parts = sb("k_parts", [P, 2, 2, CB, 2 * P], f16)
            q_ps = own.enter_context(nc.psum_tensor("q_ps", [P, 2, KV, P], f32))
            k_ps = own.enter_context(nc.psum_tensor("k_ps", [P, 2, 4, P], f32))

            x_in = [sem("x_in0"), sem("x_in1")]
            split_out = [sem("split_out0"), sem("split_out1")]
            stats_done, mv_done, var_ready = sem("stats_done"), sem("mv_done"), sem("var_ready")
            rstd_done, xn_done = sem("rstd_done"), sem("xn_done")
            turned, high_done, low_done = sem("turned"), sem("high_done"), sem("low_done")
            block = own.enter_context(nc.Block())

            def batches(eng, body):
                body(0)
                with eng.Fori(1, B) as b:
                    body(b)

            @block.sync
            def _(sp):
                def load(b, t):
                    n = ST * b + t
                    wait(sp, xn_done, n - 1)
                    wait(sp, turned, n - 1)
                    sp.dma_start(xin[:, t % 2, :], x[bass.ds(b, 1), t * P:(t + 1) * P, :]
                                 .rearrange("o p e -> (o p) e")).then_inc(x_in[t % 2], 16)
                    sp.dma_start(cin[:, t % 2, :], ctx_in[bass.ds(b, 1), t * P:(t + 1) * P, :]
                                 .rearrange("o p e -> (o p) e")).then_inc(x_in[t % 2], 16)

                def store(b, pair):
                    n = ST * b + 2 * pair
                    wait(sp, low_done, 2 * n + 4)
                    cols = slice(2 * pair * P, (2 * pair + 2) * P)
                    sp.dma_start(q_scr[bass.ds(b, 1), :, :, :, cols].rearrange("o l h p s -> p (o l h) s"),
                                 q_parts[:, pair].rearrange("p l h s -> p (l h) s")
                                 ).then_inc(split_out[pair], 16)
                    sp.dma_start(k_scr[bass.ds(b, 1), :, :, :, cols].rearrange("o l h p s -> p (o l h) s"),
                                 k_parts[:, pair].rearrange("p l h s -> p (l h) s")
                                 ).then_inc(split_out[pair], 16)

                def body(b):
                    for t in range(ST):
                        load(b, t)
                        if t == 1 and (not isinstance(b, int) or b > 0):
                            store(b - 1, 1)
                        if t == 3:
                            store(b, 0)

                batches(sp, body)
                store(B - 1, 1)
                for pair in range(2):
                    sp.wait_ge(split_out[pair], 32 * B)

            @block.gpsimd
            def _(pool):
                pool.memset(ident[:], 0.0).then_inc(ident_set, 1)
                pool.memset(ones[:], 1.0).then_inc(consts_set, 1)
                pool.memset(power[:], -0.5).then_inc(consts_set, 1)
                pool.wait_ge(ident_set, 1)
                pool.affine_select(out=ident[:], in_=ident[:], compare_op=ALU.not_equal, fill=1.0,
                                   base=0, pattern=[[-1, P]], channel_multiplier=1
                                   ).then_inc(consts_set, 1)
                pool.wait_ge(consts_set, 3)

                def body(b):
                    for t in range(ST):
                        n, k = ST * b + t, t % 2
                        wait(pool, var_ready, n + 1)
                        wait(pool, xn_done, n - 1)
                        pool.tensor_tensor(rstd[:, k:k + 1], var_eps[:, k:k + 1], power[:], ALU.pow
                                           ).then_inc(rstd_done, 1)

                batches(pool, body)

            @block.vector
            def _(dve):
                def low(out, ps, high, n, which):
                    wait(dve, high_done, 2 * n + 1 + which)
                    dve.scalar_tensor_tensor(out=out, in0=ps, scalar=UP, in1=high, op0=ALU.mult,
                                             op1=ALU.subtract).then_inc(low_done, 1)

                def low_q(n, t):
                    k, pair, cols = t % 2, t // 2 % 2, slice(t % 2 * P, (t % 2 + 1) * P)
                    low(q_parts[:, pair, 1, :, cols], q_ps[:, k], q_parts[:, pair, 0, :, cols], n, 0)

                def low_k(n, t):
                    k, pair, cols = t % 2, t // 2 % 2, slice(t % 2 * P, (t % 2 + 1) * P)
                    low(k_parts[:, pair, 1, :, cols], k_ps[:, k, 0:CB], k_parts[:, pair, 0, :, cols], n, 1)

                def body(b):
                    for t in range(ST):
                        n, k = ST * b + t, t % 2
                        before = not isinstance(n, int) or n > 0
                        dve.wait_ge(x_in[k], 32 * (2 * b + t // 2 + 1))
                        dve.bn_stats(stats[:, k, 0, :], xin[:, k, 0:512])
                        dve.bn_stats(stats[:, k, 1, :], xin[:, k, 512:1024]).then_inc(stats_done, 1)
                        dve.wait_ge(stats_done, n + 1)
                        if before:
                            low_q(n - 1, t + 3)
                        dve.bn_aggr(mv[:, k, :], stats[:, k]).then_inc(mv_done, 1)
                        dve.wait_ge(mv_done, n + 1)
                        dve.tensor_scalar_add(var_eps[:, k:k + 1], mv[:, k, 1:2], EPS
                                              ).then_inc(var_ready, 1)
                        if before:
                            low_k(n - 1, t + 3)
                        dve.wait_ge(rstd_done, n + 1)
                        wait(dve, turned, n - 1)
                        dve.tensor_scalar(xn[:, k, :], xin[:, k, :], mv[:, k, 0:1], rstd[:, k:k + 1],
                                          ALU.subtract, ALU.mult).then_inc(xn_done, 1)

                batches(dve, body)
                low_q(TILES - 1, ST - 1)
                low_k(TILES - 1, ST - 1)

            @block.tensor
            def _(pe):
                pe.wait_ge(consts_set, 3)

                def body(b):
                    for t in range(ST):
                        n, k = ST * b + t, t % 2
                        pe.wait_ge(xn_done, n + 1)
                        wait(pe, low_done, 2 * n - 2)
                        for h in range(KV):
                            pe.transpose(q_ps[:, k, h, :], xn[:, k, h * P:(h + 1) * P], ident[:])
                        for c in range(CB):
                            last = pe.transpose(k_ps[:, k, c, :], cin[:, k, c * P:(c + 1) * P], ident[:])
                        last.then_inc(turned, 1)

                batches(pe, body)

            @block.scalar
            def _(act):
                def body(b):
                    for t in range(ST):
                        n, k, pair, half = ST * b + t, t % 2, t // 2, t % 2
                        cols = slice(half * P, (half + 1) * P)
                        act.wait_ge(turned, n + 1)
                        if half == 0:
                            wait(act, split_out[pair], 32 * b)
                        act.activation(q_parts[:, pair, 0, :, cols], q_ps[:, k], ACT.Copy, scale=UP
                                       ).then_inc(high_done, 1)
                        act.activation(k_parts[:, pair, 0, :, cols], k_ps[:, k, 0:CB], ACT.Copy, scale=UP
                                       ).then_inc(high_done, 1)

                batches(act, body)

        with ExitStack() as own:
            sb = lambda name, shape, dt: own.enter_context(nc.sbuf_tensor(name, shape, dt))
            SLOTS = 4
            q_stack = sb("q_stack", [STACK, SLOTS, G, S], f16)
            k_stack = sb("k_stack", [STACK, SLOTS, S], f16)
            row_max = sb("row_max", [P, 2, G * ST], f32)
            shift = sb("shift", [G * ST, 2, 2, P], f16)
            v_in = sb("v_in", [P, 2, ST, D], f32)
            x_res = sb("x_res", [P, 2, ST, P], f32)
            x_att = sb("x_att", [P, 2, ST, P], f32)
            probs = sb("probs", [P, 2, ST, G, S], f32)
            sums = sb("sums", [P, 2, 2, G, S], f32)
            o_raw = sb("o_raw", [P, 2, S], f32)
            den_t = sb("den_t", [P, S], f32)
            inv_t = sb("inv_t", [P, S // D], f32)
            inv = sb("inv", [P, S], f32)
            o_norm = sb("o_norm", [P, S], f32)
            s_ps = own.enter_context(nc.psum_tensor("s_ps", [P, 2, 2, S], f32))
            st_ps = own.enter_context(nc.psum_tensor("st_ps", [P, 2, S], f32))
            o_ps = own.enter_context(nc.psum_tensor("o_ps", [P, S], f32))
            turn_ps = own.enter_context(nc.psum_tensor("turn_ps", [P, S], f32))

            s_in = [sem(f"s_in{i}") for i in range(SLOTS)]
            shift_in = [sem("shift_in0"), sem("shift_in1")]
            v_sem = [sem("v_in0"), sem("v_in1")]
            res_in = [sem("res_in0"), sem("res_in1")]
            a_out = [sem("a_out0"), sem("a_out1")]
            max_scored, reduced, max_turned = sem("max_scored"), sem("reduced"), sem("max_turned")
            shift_high, shift_low = sem("shift_high"), sem("shift_low")
            scored, exped, pv_done = sem("scored"), sem("exped"), sem("pv_done")
            front_done, back_done = sem("front_done"), sem("back_done")
            den_done, o_copied, o_turned = sem("den_done"), sem("o_copied"), sem("o_turned")
            den_turned, inv_made, inv_spread = sem("den_turned"), sem("inv_made"), sem("inv_spread")
            o_normed, res_added, rows_set = sem("o_normed"), sem("res_added"), sem("rows_set")
            block = own.enter_context(nc.Block())

            NMC = G * ST // 2
            NSC = ST * G
            LEAD = 4
            live = lambda u: not isinstance(u, int) or 0 <= u < UNITS

            def steps(eng, body):
                def step(j, k):
                    def at(i):
                        jj, kk = j + (k + i) // SLOTS, (k + i) % SLOTS
                        return (SLOTS * jj + kk, jj // (KV // SLOTS),
                                jj % (KV // SLOTS) * SLOTS + kk)
                    body(SLOTS * j + k, k, at)

                for j in (-1, 0):
                    for k in range(SLOTS):
                        step(j, k)
                with eng.Fori(1, UNITS // SLOTS - 1) as j:
                    for k in range(SLOTS):
                        step(j, k)
                for u in range(UNITS - SLOTS, UNITS + 2):
                    step(u // SLOTS, u % SLOTS)

            @block.gpsimd
            def _(pool):
                pool.memset(k_stack[NP3:STACK], SHIFT_UNIT).then_inc(rows_set, 1)

                def body(u, k, at):
                    if live(u):
                        wait(pool, exped, NSC * (u + 1))
                        wait(pool, den_done, u - 1)
                        pool.tensor_tensor(sums[:, k % 2, 1], probs[:, k % 2, 2], probs[:, k % 2, 3],
                                           ALU.add).then_inc(back_done, 1)
                    if live(u + 1):
                        s = (k + 1) % 2
                        wait(pool, exped, NSC * (u + 1) + NSC // 2)
                        wait(pool, den_done, u)
                        pool.tensor_tensor(sums[:, s, 0], probs[:, s, 0], probs[:, s, 1], ALU.add
                                           ).then_inc(front_done, 1)

                steps(pool, body)

            @block.sync
            def _(sp):
                def body(u, k, at):
                    if live(u + 1):
                        v, b, h = at(1)
                        s = (k + 1) % 2
                        wait(sp, pv_done, ST * (v - 1))
                        sp.dma_start(v_in[:, s], ctx_in[bass.ds(b, 1), :, bass.ds(h * D, D)]
                                     .rearrange("o (t p) d -> p (o t) d", p=P)).then_inc(v_sem[s], 16)
                    if live(u):
                        v, b, h = at(0)
                        wait(sp, res_added, v - 1)
                        sp.dma_start(x_res[:, k % 2], x[bass.ds(b, 1), :, bass.ds(h * P, P)]
                                     .rearrange("o (t p) e -> p (o t) e", p=P)).then_inc(res_in[k % 2], 16)
                    if live(u - 2):
                        v, b, h = at(-2)
                        wait(sp, res_added, v + 1)
                        sp.dma_start(y_scr[bass.ds(b, 1), :, bass.ds(h * P, P)]
                                     .rearrange("o (t p) e -> p (o t) e", p=P), x_att[:, k % 2]
                                     ).then_inc(a_out[k % 2], 16)
                    if live(u + LEAD):
                        v, b, h = at(LEAD)
                        wait(sp, scored, NSC * (v - 3))
                        of_q = q_scr[bass.ds(b, 1), :, bass.ds(h, 1), :, :].rearrange(
                            "o l c (g d) s -> d (o c l) g s", d=D)
                        for row, part in enumerate((0, 0, 1)):
                            sp.dma_start(q_stack[row * D:(row + 1) * D, k], of_q[:, part]
                                         ).then_inc(s_in[k], 16)
                        of_k = k_scr[bass.ds(b, 1), :, bass.ds(h // SLOTS, 1),
                                     k * D:(k + 1) * D, :].rearrange("o l c d s -> d (o c l) s")
                        for row, part in enumerate((0, 1, 0)):
                            sp.dma_start(k_stack[row * D:(row + 1) * D, k], of_k[:, part]
                                         ).then_inc(s_in[k], 16)
                    if live(u + 2):
                        v, s = u + 2, k % 2
                        wait(sp, shift_low, v + 1)
                        for part in range(2):
                            sp.dma_start(q_stack[NP3 + part:NP3 + part + 1, (k + 2) % SLOTS]
                                         .rearrange("r g s -> r (g s)"), shift[:, s, part, :]
                                         ).then_inc(shift_in[s], 16)

                steps(sp, body)
                for s in range(2):
                    sp.wait_ge(a_out[s], 16 * (UNITS // 2))

            @block.tensor
            def _(pe):
                pe.wait_ge(rows_set, 1)

                def score_rows(u, k, c):
                    for i in range(2):
                        g, t = (2 * c + i) // ST, (2 * c + i) % ST
                        last = pe.matmul(s_ps[:, c % 2, i, :], q_stack[0:NP3, k, g, t * P:(t + 1) * P],
                                         k_stack[0:NP3, k, :], start=True, stop=True)
                    last.then_inc(max_scored, 1)

                def body(u, k, at):
                    k3, k1 = (k + 3) % SLOTS, (k + 1) % SLOTS
                    def score_pair(t, pair):
                        if t == 0 and pair == 0:
                            wait(pe, shift_in[k1 % 2], 32 * (at(1)[0] // 2 + 1))
                        for g in (2 * pair, 2 * pair + 1):
                            n = t * G + g
                            wait(pe, exped, NSC * (u + 1) + n - 1)
                            pe.matmul(st_ps[:, n % 2, :], k_stack[:, k1, t * P:(t + 1) * P],
                                      q_stack[:, k1, g, :], start=True, stop=True).then_inc(scored, 1)

                    for t in range(ST):
                        if live(u + 1):
                            score_pair(t, 0)
                        if live(u + 3):
                            if t == 0:
                                wait(pe, s_in[k3], 96 * (at(3)[0] // SLOTS + 1))
                            for c in (2 * t, 2 * t + 1):
                                wait(pe, reduced, NMC * (u + 3) + c - 1)
                                score_rows(u + 3, k3, c)
                        if live(u + 1):
                            score_pair(t, 1)
                        if live(u):
                            s = k % 2
                            if t == 0:
                                wait(pe, v_sem[s], 16 * (at(0)[0] // 2 + 1))
                                wait(pe, o_copied, u)
                                wait(pe, exped, NSC * (u + 1))
                            for g in range(G):
                                last = pe.matmul(o_ps[g * D:(g + 1) * D, :], v_in[:, s, t, :],
                                                 probs[:, s, t, g, :], start=(t == 0), stop=(t == ST - 1))
                            last.then_inc(pv_done, 1)
                        if t == 0 and live(u - 1):
                            wait(pe, front_done, u)
                            wait(pe, back_done, u)
                            wait(pe, res_added, u - 1)
                            for g in range(G):
                                for half in range(2):
                                    last = pe.matmul(turn_ps[g * D:(g + 1) * D, :], ones[:, 0:D],
                                                     sums[:, (k + 1) % 2, half, g, :],
                                                     start=(half == 0), stop=(half == 1))
                            last.then_inc(den_done, 1)
                        if t == 1 and live(u + 2):
                            wait(pe, reduced, NMC * (u + 3))
                            wait(pe, den_turned, u)
                            pe.transpose(turn_ps[0:G * ST, 0:P], row_max[:, k % 2, :], ident[:]
                                         ).then_inc(max_turned, 1)
                        if t == 2 and live(u - 1):
                            wait(pe, o_normed, u)
                            wait(pe, shift_low, min(u + 3, UNITS) if isinstance(u, int) else u + 3)
                            for i in range(ST):
                                last = pe.transpose(turn_ps[:, i * P:(i + 1) * P],
                                                    o_norm[:, i * P:(i + 1) * P], ident[:])
                            last.then_inc(o_turned, 1)

                steps(pe, body)

            @block.scalar
            def _(act):
                def body(u, k, at):
                    if live(u - 1):
                        wait(act, pv_done, ST * u)
                        wait(act, o_normed, u - 2)
                        act.activation(o_raw[:, (k + 1) % 2, :], o_ps[:], ACT.Copy).then_inc(o_copied, 1)
                    for t in range(ST):
                        if live(u + 1):
                            s = (k + 1) % 2
                            wait(act, pv_done, ST * (u - 1) + t + 1)
                            wait(act, front_done if t < ST // 2 else back_done, u)
                            for g in range(G):
                                n = t * G + g
                                wait(act, scored, NSC * (u + 1) + n + 1)
                                act.activation(probs[:, s, t, g, :], st_ps[:, n % 2, :], ACT.Exp,
                                               scale=EXP_SCALE).then_inc(exped, 1)
                        if t == 1 and live(u + 2):
                            wait(act, max_turned, u + 3)
                            wait(act, shift_in[k % 2], 32 * (at(2)[0] // 2))
                            act.activation(shift[:, k % 2, 0, :], turn_ps[0:G * ST, 0:P], ACT.Copy,
                                           scale=-1.0 / SHIFT_UNIT).then_inc(shift_high, 1)

                steps(act, body)

            @block.vector
            def _(dve):
                def body(u, k, at):
                    s = (k + 1) % 2
                    for c in range(NMC):
                        if live(u + 3):
                            if c == 0:
                                wait(dve, max_turned, u + 2)
                            wait(dve, max_scored, NMC * (u + 3) + c + 1)
                            dve.reduce_max(row_max[:, s, 2 * c:2 * c + 2], s_ps[:, c % 2], AX.X
                                           ).then_inc(reduced, 1)
                        if live(u - 1):
                            if c == 1:
                                wait(dve, den_done, u)
                                dve.transpose(den_t[:], turn_ps[:]).then_inc(den_turned, 1)
                            if c == 2:
                                wait(dve, den_turned, u)
                                dve.reciprocal(inv_t[:], den_t[:, 0:S:D]).then_inc(inv_made, 1)
                            if c == 3:
                                wait(dve, inv_made, u)
                                dve.transpose(inv[:].rearrange("p (a b) -> p a b", b=D),
                                              inv_t[:].unsqueeze(2).to_broadcast([P, S // D, D])
                                              ).then_inc(inv_spread, 1)
                            if c == 4:
                                wait(dve, inv_spread, u)
                                wait(dve, o_copied, u)
                                wait(dve, o_turned, u - 1)
                                dve.tensor_tensor(o_norm[:], o_raw[:, s, :], inv[:], ALU.mult
                                                  ).then_inc(o_normed, 1)
                        if c == 4 and live(u + 2):
                            wait(dve, shift_high, u + 3)
                            dve.scalar_tensor_tensor(out=shift[:, k % 2, 1, :], in0=turn_ps[0:G * ST, 0:P],
                                                     scalar=-1.0 / SHIFT_UNIT, in1=shift[:, k % 2, 0, :],
                                                     op0=ALU.mult, op1=ALU.subtract).then_inc(shift_low, 1)
                        if c == 6 and live(u - 1):
                            wait(dve, o_turned, u)
                            wait(dve, res_in[s], 16 * (at(-1)[0] // 2 + 1))
                            wait(dve, a_out[s], 16 * (at(-1)[0] // 2))
                            dve.tensor_tensor(x_att[:, s].rearrange("p t e -> p (t e)"),
                                              x_res[:, s].rearrange("p t e -> p (t e)"), turn_ps[:],
                                              ALU.add).then_inc(res_added, 1)

                steps(dve, body)

        with ExitStack() as own:
            sb = lambda name, shape, dt: own.enter_context(nc.sbuf_tensor(name, shape, dt))
            sel_sb = sb("sel_sb", [P, NX, EC, NS], f32)
            upd_sb = sb("upd_sb", [P, NX, EC, NS], f32)
            deg_sb = sb("deg_sb", [P, NX, EC, NS], f32)
            deg_cols = sb("deg_cols", [P, EC, NE], f32)
            mu_sb = sb("mu_sb", [P, NX, EC], f32)
            deb_sb = sb("deb_sb", [P, NX, EC], f32)
            w_all = sb("w_all", [P, EC, WC], f32)
            down = sb("down", [P, E], f32)
            prod = sb("prod", [P, 3, NX, NS, EC], f32)
            c_part = sb("c_part", [P, WC + 2 * NX], f32)
            cst = sb("cst", [P, WC + 2 * NX], f32)
            neg_slope = sb("neg_slope", [P, NX], f32)
            rank = sb("rank", [P, NX], f32)
            xa = sb("xa", [P, 2, ST, E], f32)
            y = sb("y", [P, 2, E], f32)
            yT = sb("yT", [P, EC, P], f32)
            xy = sb("xy", [P, 2, E], f32)
            x_out = sb("x_out", [P, ST, E], f32)
            mixT = sb("mixT", [P, ST, P], f32)
            mix = sb("mix", [P, ST, P], f32)
            stats = sb("stats3", [P, 2, 6], f32)
            mv = sb("mv3", [P, 2, ST, 2], f32)
            var_eps = sb("var_eps3", [P, 1], f32)
            rstd = sb("rstd3", [P, 2, ST], f32)
            neg_mr = sb("neg_mr", [P, 2, ST], f32)
            y_sq = sb("y_sq", [P, 2, ST], f32)
            z_sb = sb("z_sb", [P, ST, WC], f32)
            sq = sb("sq", [P, ST, NE], f32)
            rows = sb("rows", [P, 13, ST, NX], f32)
            top = sb("top", [P, 2, ST], f32)
            z_e = sb("z_e", [P, ST, NX], f32)
            x_scale = sb("x_scale", [P, ST], f32)
            x_bias = sb("x_bias", [P, ST], f32)
            y_ps = own.enter_context(nc.psum_tensor("y_ps", [P, EC, P], f32))
            z_ps = own.enter_context(nc.psum_tensor("z_ps", [P, 2, 512], f32))
            mix_ps = own.enter_context(nc.psum_tensor("mix_ps", [P, ST, P], f32))
            r_ps = own.enter_context(nc.psum_tensor("r_ps", [P, E], f32))

            w_in, zeroed, prep, folded = sem("w_in"), sem("zeroed"), sem("prep"), sem("folded")
            down_turned, down_copied, cst_done = sem("down_turned"), sem("down_copied"), sem("cst_done")
            t_in = [sem(f"t_in{i}") for i in range(2 * ST)]
            t_out = [sem(f"t_out{i}") for i in range(ST)]
            ln_chain, gate_chain, xy_done = sem("ln_chain"), sem("gate_chain"), sem("xy_done")
            var_ready, rstd_done, y_done = sem("var_ready3"), sem("rstd_done3"), sem("y_done")
            y_turned, yT_done, z_done = sem("y_turned"), sem("yT_done"), sem("z_done")
            z_read, e_ready, e_done, mix_done = sem("z_read"), sem("e_ready"), sem("e_done"), sem("mix_done")
            mix_turned, mixT_done, r_done, final = sem("mix_turned"), sem("mixT_done"), sem("r_done"), sem("final")
            block = own.enter_context(nc.Block())

            def steps(eng, body):
                body(0, 0, True, False)
                body(1, 1, True, True)
                with eng.Fori(1, B // 2 - 1) as j:
                    for k in range(2):
                        body(2 * j + k, k, True, True)
                for q in range(B - 2, B + 1):
                    body(q, q % 2, q < B, True)

            x_tiles = y_scr.rearrange("b (t p) e -> (b t) p e", p=P)
            o_tiles = out.rearrange("b (t p) e -> (b t) p e", p=P)

            @block.sync
            def _(sp):
                for dst, src in ((sel_sb, sel_w), (upd_sb, lora_up), (deg_sb, lora_dn)):
                    sp.dma_start(dst[:].rearrange("p n c s -> p n (c s)"),
                                 src.rearrange("n (p c) s -> p n (c s)", c=EC)).then_inc(w_in, 16)
                sp.dma_start(mu_sb[:], sel_mu.rearrange("n (p c) -> p n c", c=EC)).then_inc(w_in, 16)
                sp.dma_start(deb_sb[:], debias_w.rearrange("n (p c) -> p n c", c=EC)).then_inc(w_in, 16)

                def load(q, k, t):
                    sp.dma_start(xa[:, k, t, :], x_tiles[bass.ds(ST * q + t, 1)].rearrange("o p e -> (o p) e")
                                 ).then_inc(t_in[ST * k + t], 16)

                for t in range(ST):
                    load(0, 0, t)
                sp.wait_ge(zeroed, 3)
                sp.dma_start(down[NE:NE + NX, :], bias_w).then_inc(w_in, 16)
                sp.dma_start(c_part[0:1, WC:WC + NX], imp_center.rearrange("(o n) -> o n", o=1)).then_inc(w_in, 16)
                sp.dma_start(c_part[0:1, WC + NX:], imp_slope.rearrange("(o n) -> o n", o=1)).then_inc(w_in, 16)
                for t in range(ST):
                    load(1, 1, t)

                def body(q, k, more, before):
                    for t in range(ST):
                        if before:
                            if not isinstance(q, int) or q + 1 < B:
                                sp.wait_ge(xy_done, ST * (q - 1) + t + 1)
                                load(q + 1, 1 - k, t)
                            sp.wait_ge(final, ST * (q - 1) + t + 1)
                            sp.dma_start(o_tiles[bass.ds(ST * (q - 1) + t, 1)].rearrange("o p e -> (o p) e"),
                                         x_out[:, t, :]).then_inc(t_out[t], 16)

                steps(sp, body)
                for t in range(ST):
                    sp.wait_ge(t_out[t], 16 * B)

            @block.gpsimd
            def _(pool):
                pool.memset(c_part[:], 0.0).then_inc(zeroed, 1)
                pool.memset(down[:], 0.0).then_inc(zeroed, 1)
                pool.memset(mix[:], 0.0).then_inc(zeroed, 1)
                for n in range(NX):
                    pool.memset(rank[:, n:n + 1], float(NX - n)).then_inc(zeroed, 1)

                def body(q, k, more, before):
                    for t in range(ST):
                        if more:
                            wait(pool, var_ready, ST * q + t + 1)
                            wait(pool, mix_done, q - 1)
                            pool.tensor_tensor(rstd[:, k, t:t + 1], var_eps[:], power[:], ALU.pow
                                               ).then_inc(rstd_done, 1)

                steps(pool, body)

            @block.tensor
            def _(pe):
                pe.wait_ge(prep, 1)
                for half in range(2):
                    if half:
                        pe.wait_ge(down_copied, 1)
                    for i in range(4):
                        last = pe.transpose(mix_ps[0:NE, i, :], deg_cols[:, 4 * half + i, :], ident[:])
                    last.then_inc(down_turned, 1)
                pe.wait_ge(prep, 5)
                pe.matmul(z_ps[:, 0, 0:WC + 2 * NX], ones[:], c_part[:], start=True, stop=True
                          ).then_inc(folded, 1)
                pe.wait_ge(cst_done, 2)

                def turn(q, t):
                    n = ST * q + t
                    wait(pe, y_done, n + 1)
                    wait(pe, yT_done, n)
                    for c in range(EC):
                        last = pe.transpose(y_ps[:, c, :], y[:, t % 2, c:E:EC], ident[:])
                    last.then_inc(y_turned, 1)

                def project(q, t):
                    n = ST * q + t
                    wait(pe, yT_done, n + 1)
                    wait(pe, z_read, n - 1)
                    for c in range(EC):
                        last = pe.matmul(z_ps[:, t % 2, 0:WC], yT[:, c, :], w_all[:, c, :],
                                         start=(c == 0), stop=(c == EC - 1))
                    last.then_inc(z_done, 1)

                def turn_mix(q):
                    wait(pe, mix_done, q + 1)
                    wait(pe, mixT_done, q)
                    for t in range(ST):
                        last = pe.transpose(mix_ps[:, t, :], mix[:, t, :], ident[:])
                    last.then_inc(mix_turned, 1)

                def result(q, t):
                    n = ST * q + t
                    wait(pe, mixT_done, q + 1)
                    wait(pe, final, n)
                    for half in range(2):
                        last = pe.matmul(r_ps[:, half * 512:(half + 1) * 512], mixT[:, t, :],
                                         down[:, half * 512:(half + 1) * 512], start=True, stop=True)
                    last.then_inc(r_done, 1)

                def body(q, k, more, before):
                    if more:
                        turn(q, 0)
                        project(q, 0)
                    if before:
                        turn_mix(q - 1)
                    for t in range(1, ST):
                        if more:
                            turn(q, t)
                        if before:
                            result(q - 1, t - 1)
                        if more:
                            project(q, t)
                    if before:
                        result(q - 1, ST - 1)

                steps(pe, body)

            @block.scalar
            def _(act):
                act.wait_ge(zeroed, 2)
                for half in range(2):
                    act.wait_ge(down_turned, half + 1)
                    act.activation(down[0:NE, :].rearrange("m (p c) -> m c p", c=EC)[:, 4 * half:4 * half + 4, :],
                                   mix_ps[0:NE], ACT.Copy).then_inc(down_copied, 1)
                act.wait_ge(folded, 1)
                act.activation(cst[:], z_ps[:, 0, 0:WC + 2 * NX], ACT.Copy).then_inc(cst_done, 1)
                act.wait_ge(cst_done, 1)
                act.activation(neg_slope[:], cst[:, WC + NX:], ACT.Copy, scale=-1.0).then_inc(cst_done, 1)

                def copy_yT(q, t):
                    n = ST * q + t
                    wait(act, y_turned, n + 1)
                    wait(act, z_done, n)
                    act.activation(yT[:], y_ps[:], ACT.Copy).then_inc(yT_done, 1)

                def skip(q, k, t):
                    n = ST * q + t
                    wait(act, final, n - 1)
                    wait(act, mix_done, q + 1)
                    act.activation(xy[:, t % 2, :], xa[:, k, t, :], ACT.Identity,
                                   scale=x_scale[:, t:t + 1], bias=x_bias[:, t:t + 1]).then_inc(xy_done, 1)

                def body(q, k, more, before):
                    if more:
                        copy_yT(q, 0)
                    if before:
                        wait(act, e_ready, q)
                        act.activation(z_e[:], rows[:, 7], ACT.Exp).then_inc(e_done, 1)
                        wait(act, mix_turned, q)
                        act.activation(mixT[:], mix_ps[:], ACT.Copy).then_inc(mixT_done, 1)
                    for t in range(1, ST):
                        if more:
                            copy_yT(q, t)
                        if before:
                            skip(q - 1, 1 - k, t - 1)
                    if before:
                        skip(q - 1, 1 - k, ST - 1)

                steps(act, body)

            @block.vector
            def _(dve):
                dve.wait_ge(w_in, 128)
                dve.wait_ge(zeroed, 3 + NX)
                for n, w in enumerate((sel_sb, upd_sb)):
                    dve.tensor_copy(w_all[:, :, n * NE:(n + 1) * NE].rearrange("p c (n s) -> p c n s", n=NX),
                                    w[:].rearrange("p n c s -> p c n s"))
                dve.tensor_copy(deg_cols[:].rearrange("p c (n s) -> p c n s", n=NX),
                                deg_sb[:].rearrange("p n c s -> p c n s"))
                dve.tensor_scalar(w_all[:, :, 2 * NE:], mu_sb[:].rearrange("p n c -> p c n"), -2.0, None,
                                  ALU.mult).then_inc(prep, 1)
                for n, (w, m) in enumerate(((sel_sb, mu_sb), (upd_sb, deb_sb))):
                    dve.tensor_tensor(prod[:, n], w[:].rearrange("p n c s -> p n s c"),
                                      m[:].unsqueeze(2).to_broadcast([P, NX, NS, EC]), ALU.mult)
                dve.scalar_tensor_tensor(out=prod[:, 2, :, 0, :], in0=mu_sb[:], scalar=-1.0, in1=mu_sb[:],
                                         op0=ALU.mult, op1=ALU.mult).then_inc(prep, 1)
                dve.wait_ge(prep, 2)
                for n in range(2):
                    dve.reduce_sum(c_part[:, n * NE:(n + 1) * NE],
                                   prod[:, n].rearrange("p n s c -> p (n s) c"), AX.X).then_inc(prep, 1)
                dve.reduce_sum(c_part[:, 2 * NE:WC], prod[:, 2, :, 0, :], AX.X).then_inc(prep, 1)
                dve.wait_ge(cst_done, 2)

                LN = 3
                GATE = 15

                def normalise(q, k, t, between):
                    n = ST * q + t
                    wait(dve, t_in[ST * k + t], 16 * ((q - k) // 2 + 1))
                    dve.bn_stats(stats[:, 0, :], xa[:, k, t, 0:512])
                    dve.bn_stats(stats[:, 1, :], xa[:, k, t, 512:1024]).then_inc(ln_chain, 1)
                    dve.wait_ge(ln_chain, LN * n + 1)
                    between()
                    dve.bn_aggr(mv[:, k, t, :], stats[:]).then_inc(ln_chain, 1)
                    dve.wait_ge(ln_chain, LN * n + 2)
                    wait(dve, rstd_done, n)
                    dve.tensor_scalar_add(var_eps[:], mv[:, k, t, 1:2], EPS).then_inc(var_ready, 1)
                    dve.wait_ge(rstd_done, n + 1)
                    wait(dve, y_turned, n - 1)
                    dve.tensor_scalar(y[:, t % 2, :], xa[:, k, t, :], mv[:, k, t, 0:1], rstd[:, k, t:t + 1],
                                      ALU.subtract, ALU.mult).then_inc(y_done, 1)
                    dve.scalar_tensor_tensor(out=y_sq[:, k, t:t + 1], in0=rstd[:, k, t:t + 1],
                                             scalar=mv[:, k, t, 1:2], in1=rstd[:, k, t:t + 1], op0=ALU.mult,
                                             op1=ALU.mult).then_inc(ln_chain, 1)

                def read_z(q, t):
                    n = ST * q + t
                    wait(dve, z_done, n + 1)
                    dve.tensor_tensor(z_sb[:, t, :], z_ps[:, t % 2, 0:WC], cst[:, 0:WC], ALU.subtract
                                      ).then_inc(z_read, 1)

                def gates(q, k):
                    count = [0]
                    row = lambda j: rows[:, j]
                    over = lambda v: v.unsqueeze(1).to_broadcast([P, ST, NX])
                    each = lambda v: v.unsqueeze(2).to_broadcast([P, ST, NX])

                    def link(ins):
                        count[0] += 1
                        ins.then_inc(gate_chain, 1)
                        dve.wait_ge(gate_chain, GATE * q + count[0])

                    dve.wait_ge(z_read, ST * (q + 1))
                    dve.tensor_tensor(sq[:], z_sb[:, :, 0:NE], z_sb[:, :, 0:NE], ALU.mult)
                    dve.wait_ge(ln_chain, LN * ST * (q + 1))
                    link(dve.tensor_scalar(row(0)[:, :, 0], y_sq[:, k, :], float(E), None, ALU.mult))
                    link(dve.tensor_tensor(row(1), z_sb[:, :, 2 * NE:], each(row(0)[:, :, 0]), ALU.add))
                    dve.reduce_sum(row(2).rearrange("p t n -> p (t n)"),
                                   sq[:].rearrange("p t (n s) -> p (t n) s", n=NX), AX.X)
                    link(dve.reciprocal(row(3), row(1)))
                    link(dve.tensor_tensor(row(4), row(2), row(3), ALU.mult))
                    link(dve.tensor_tensor(row(5), row(4), over(cst[:, WC:WC + NX]), ALU.subtract))
                    link(dve.tensor_tensor(row(6), row(5), over(neg_slope[:]), ALU.mult))
                    dve.tensor_scalar_min(row(7), row(6), 87.0).then_inc(e_ready, 1)
                    dve.scalar_tensor_tensor(out=neg_mr[:, k, :], in0=mv[:, k, :, 0], scalar=-1.0,
                                             in1=rstd[:, k, :], op0=ALU.mult, op1=ALU.mult)
                    dve.wait_ge(e_done, q + 1)
                    link(dve.tensor_scalar_add(row(8), z_e[:], 1.0))
                    link(dve.reciprocal(row(9), row(8)))
                    link(dve.reduce_max(top[:, 0, :], row(9), AX.X))
                    link(dve.tensor_tensor(row(10), row(9), each(top[:, 0, :]), ALU.is_ge))
                    link(dve.tensor_tensor(row(11), row(10), over(rank[:]), ALU.mult))
                    wait(dve, xy_done, ST * q)
                    dve.tensor_scalar(x_bias[:], top[:, 0, :], -1.0, 1.0, ALU.mult, ALU.add)
                    link(dve.reduce_max(top[:, 1, :], row(11), AX.X))
                    link(dve.tensor_tensor(row(12), row(11), each(top[:, 1, :]), ALU.is_equal))
                    dve.tensor_tensor(x_scale[:], x_bias[:], rstd[:, k, :], ALU.mult)
                    wait(dve, mix_turned, q)
                    link(dve.tensor_tensor(mix[:, :, NE:NE + NX], row(12), each(top[:, 0, :]), ALU.mult))
                    dve.tensor_tensor(x_bias[:], x_bias[:], neg_mr[:, k, :], ALU.mult)
                    link(dve.tensor_scalar_add(x_scale[:], x_scale[:], 1.0))
                    dve.tensor_tensor(mix[:, :, 0:NE].rearrange("p t (n s) -> p t n s", n=NX),
                                      z_sb[:, :, NE:2 * NE].rearrange("p t (n s) -> p t n s", n=NX),
                                      mix[:, :, NE:NE + NX].unsqueeze(3).to_broadcast([P, ST, NX, NS]),
                                      ALU.mult).then_inc(mix_done, 1)
                    assert count[0] == GATE, count

                def finish(q, t):
                    n = ST * q + t
                    wait(dve, xy_done, n + 1)
                    wait(dve, r_done, n + 1)
                    wait(dve, t_out[t], 16 * q)
                    dve.tensor_tensor(x_out[:, t, :], xy[:, t % 2, :], r_ps[:], ALU.add).then_inc(final, 1)

                nothing = lambda: None

                def body(q, k, more, before):
                    if before:
                        if more:
                            normalise(q, k, 1, lambda: read_z(q - 1, ST - 1))
                        else:
                            read_z(q - 1, ST - 1)
                        gates(q - 1, 1 - k)
                    else:
                        normalise(q, k, 0, nothing)
                        normalise(q, k, 1, nothing)
                    for t in range(2, ST):
                        if more:
                            normalise(q, k, t, lambda: read_z(q, t - 2))
                        if before:
                            finish(q - 1, t - 2)
                    following = more and not (isinstance(q, int) and q == B - 1)
                    if following and before:
                        normalise(q + 1, 1 - k, 0, lambda: finish(q - 1, ST - 2))
                    elif following:
                        normalise(q + 1, 1 - k, 0, nothing)
                    elif before:
                        finish(q - 1, ST - 2)
                    if more:
                        read_z(q, ST - 2)
                    if before:
                        finish(q - 1, ST - 1)

                steps(dve, body)


_INS = ['x', 'ctx_512', 'L0_ffn_select_weight', 'L0_ffn_select_mean_diff', 'L0_ffn_imp_center',
        'L0_ffn_imp_slope', 'L0_ffn_lora_update', 'L0_ffn_lora_degen', 'L0_ffn_bias_w',
        'L0_ffn_debias_w']


def kernel(**inputs):
    import numpy as _np
    import concourse.bacc as _bacc
    from concourse import mybir as _mybir
    from concourse.bass_utils import run_bass_kernel_spmd as _run

    nc = _bacc.Bacc("TRN2", target_bir_lowering=False, num_devices=1)
    arrays, args = {}, []
    for name in _INS:
        a = _np.ascontiguousarray(inputs[name])
        arrays[f"in_{name}_dram"] = a
        args.append(nc.dram_tensor(f"in_{name}_dram", a.shape, _mybir.dt.from_np(a.dtype), kind="ExternalInput").ap())
    args.append(nc.dram_tensor("out_0_dram", inputs['x'].shape, _mybir.dt.float32, kind="ExternalOutput").ap())
    xattn_ffn(nc, *args)
    r = _run(nc, [arrays], core_ids=[0])
    return r.results[0]["out_0_dram"]
```

```python
import concourse.bass as bass
from concourse import mybir
from contextlib import ExitStack


def xattn_ffn(nc: bass.Bass, x, ctx_in, sel_w, sel_mu, imp_center, imp_slope, lora_up, lora_dn,
              bias_w, debias_w, out):
    f32, f16 = mybir.dt.float32, mybir.dt.float16
    ALU = mybir.AluOpType
    ACT = mybir.ActivationFunctionType
    AX = mybir.AxisListType

    P = 128
    B, S, E = x.shape
    CE = ctx_in.shape[2]
    D = 32
    KV = CE // D
    G = E // D // KV
    ST = S // P
    CB = CE // P
    NX, _, NS = sel_w.shape
    EC = E // P
    UNITS = B * KV
    TILES = B * ST
    EPS = 1e-5
    UP = 16.0
    EXP_SCALE = 1.0 / (UP * UP * D ** 0.5)
    SHIFT_UNIT = 4096.0
    NP3 = 3 * D
    STACK = NP3 + 2
    NE = NX * NS
    WC = 2 * NE + NX
    ONE_ROW = 96
    assert NE + NX <= ONE_ROW and G * D == P and S == 512 and NE + NX <= P

    q_scr = nc.dram_tensor("q_split", [B, 2, KV, P, S], f16, kind="Internal").ap()
    k_scr = nc.dram_tensor("k_split", [B, 2, CB, P, S], f16, kind="Internal").ap()
    y_scr = nc.dram_tensor("attended", [B, S, E], f32, kind="Internal").ap()

    def wait(eng, sem, count):
        if not isinstance(count, int) or count > 0:
            eng.wait_ge(sem, count)

    with ExitStack() as keep:
        sem = lambda name: keep.enter_context(nc.semaphore(name))
        ident = keep.enter_context(nc.sbuf_tensor("ident", [P, P], f32))
        ones = keep.enter_context(nc.sbuf_tensor("ones", [P, P], f32))
        power = keep.enter_context(nc.sbuf_tensor("power", [P, 1], f32))
        consts_set, ident_set = sem("consts_set"), sem("ident_set")
        SLOTS = 4
        q_stack = keep.enter_context(nc.sbuf_tensor("q_stack", [STACK, SLOTS, G, S], f16))
        k_stack = keep.enter_context(nc.sbuf_tensor("k_stack", [STACK, SLOTS, S], f16))
        s_in = [sem(f"s_in{i}") for i in range(SLOTS)]
        rows_set = sem("rows_set")

        def load_stacks(sp, b, h, slot):
            of_q = q_scr[bass.ds(b, 1), :, bass.ds(h, 1), :, :].rearrange("o l c (g d) s -> d (o c l) g s", d=D)
            for row, part in enumerate((0, 0, 1)):
                sp.dma_start(q_stack[row * D:(row + 1) * D, slot], of_q[:, part]).then_inc(s_in[slot], 16)
            of_k = k_scr[bass.ds(b, 1), :, bass.ds(h // SLOTS, 1),
                         slot * D:(slot + 1) * D, :].rearrange("o l c d s -> d (o c l) s")
            for row, part in enumerate((0, 1, 0)):
                sp.dma_start(k_stack[row * D:(row + 1) * D, slot], of_k[:, part]).then_inc(s_in[slot], 16)

        xa0 = keep.enter_context(nc.sbuf_tensor("xa0", [P, ST, E], f32))
        GROUPS = 3
        t_in = [sem(f"t_in{i}") for i in range(GROUPS * ST)]
        x_tiles = y_scr.rearrange("b (t p) e -> (b t) p e", p=P)

        kb = lambda name, shape: keep.enter_context(nc.sbuf_tensor(name, shape, f32))
        sel_sb = kb("sel_sb", [P, NX, EC, NS])
        upd_sb = kb("upd_sb", [P, NX, EC, NS])
        deg_sb = kb("deg_sb", [P, NX, EC, NS])
        deg_cols = kb("deg_cols", [P, EC, NE])
        mu_sb = kb("mu_sb", [P, NX, EC])
        deb_sb = kb("deb_sb", [P, NX, EC])
        w_all = kb("w_all", [P, EC, WC])
        down = kb("down", [P, E])
        mix = kb("mix", [P, ST, P])
        prod = kb("prod", [P, 3, NX, NS, EC])
        c_part = kb("c_part", [P, WC + 2 * NX])
        cst = kb("cst", [P, WC + 2 * NX])
        neg_slope = kb("neg_slope", [P, NX])
        rank = kb("rank", [P, NX])
        w_in, zeroed, prep, folded = sem("w_in"), sem("zeroed"), sem("prep"), sem("folded")
        down_turned, down_copied, cst_done = sem("down_turned"), sem("down_copied"), sem("cst_done")

        with ExitStack() as own:
            sb = lambda name, shape, dt: own.enter_context(nc.sbuf_tensor(name, shape, dt))
            xin = sb("xin", [P, ST, E], f32)
            cin = sb("cin", [P, ST, CE], f32)
            xn = sb("xn", [P, 2, E], f32)
            stats = sb("stats", [P, 2, 2, 6], f32)
            mv = sb("mv", [P, 2, 2], f32)
            var_eps = sb("var_eps", [P, 2], f32)
            rstd = sb("rstd", [P, 2], f32)
            q_parts = sb("q_parts", [P, 2, 2, KV, 2 * P], f16)
            k_parts = sb("k_parts", [P, 2, 2, CB, 2 * P], f16)
            q_ps = own.enter_context(nc.psum_tensor("q_ps", [P, 2, KV, P], f32))
            k_ps = own.enter_context(nc.psum_tensor("k_ps", [P, 2, 4, P], f32))

            x_in = [sem(f"x_in{t}") for t in range(ST)]
            split_out = [sem("split_out0"), sem("split_out1")]
            stats_done, mv_done, var_ready = sem("stats_done"), sem("mv_done"), sem("var_ready")
            rstd_done, xn_done = sem("rstd_done"), sem("xn_done")
            turned, high_done, low_done = sem("turned"), sem("high_done"), sem("low_done")
            block = own.enter_context(nc.Block())

            def batches(eng, body):
                body(0, False)
                with eng.Fori(1, B - 1) as b:
                    body(b, False)
                body(B - 1, True)

            @block.sync
            def _(sp):
                def load(b, t):
                    n = ST * b + t
                    wait(sp, xn_done, n - ST + 1)
                    wait(sp, turned, n - ST + 1)
                    sp.dma_start(xin[:, t, :], x[bass.ds(b, 1), t * P:(t + 1) * P, :]
                                 .rearrange("o p e -> (o p) e")).then_inc(x_in[t], 16)
                    sp.dma_start(cin[:, t, :], ctx_in[bass.ds(b, 1), t * P:(t + 1) * P, :]
                                 .rearrange("o p e -> (o p) e")).then_inc(x_in[t], 16)

                def store(b, pair):
                    n = ST * b + 2 * pair
                    wait(sp, low_done, 2 * n + 4)
                    cols = slice(2 * pair * P, (2 * pair + 2) * P)
                    sp.dma_start(q_scr[bass.ds(b, 1), :, :, :, cols].rearrange("o l h p s -> p (o l h) s"),
                                 q_parts[:, pair].rearrange("p l h s -> p (l h) s")
                                 ).then_inc(split_out[pair], 16)
                    sp.dma_start(k_scr[bass.ds(b, 1), :, :, :, cols].rearrange("o l h p s -> p (o l h) s"),
                                 k_parts[:, pair].rearrange("p l h s -> p (l h) s")
                                 ).then_inc(split_out[pair], 16)

                def body(b, last):
                    for t in range(ST):
                        if not last:
                            load(b + 1, t)
                        elif t % 2 == 0:
                            for pair in range(2):
                                sp.wait_ge(split_out[pair], 32)
                            for h in (t, t + 1):
                                load_stacks(sp, 0, h, h)
                        if t % 2 == 1:
                            store(b, t // 2)

                for t in range(ST):
                    load(0, t)
                for dst, src in ((sel_sb, sel_w), (upd_sb, lora_up), (deg_sb, lora_dn)):
                    sp.dma_start(dst[:].rearrange("p n c s -> p n (c s)"),
                                 src.rearrange("n (p c) s -> p n (c s)", c=EC)).then_inc(w_in, 16)
                sp.dma_start(mu_sb[:], sel_mu.rearrange("n (p c) -> p n c", c=EC)).then_inc(w_in, 16)
                sp.dma_start(deb_sb[:], debias_w.rearrange("n (p c) -> p n c", c=EC)).then_inc(w_in, 16)
                sp.wait_ge(zeroed, 3)
                sp.dma_start(down[NE:NE + NX, :], bias_w).then_inc(w_in, 16)
                sp.dma_start(c_part[0:1, WC:WC + NX], imp_center.rearrange("(o n) -> o n", o=1)).then_inc(w_in, 16)
                sp.dma_start(c_part[0:1, WC + NX:], imp_slope.rearrange("(o n) -> o n", o=1)).then_inc(w_in, 16)
                batches(sp, body)
                for pair in range(2):
                    sp.wait_ge(split_out[pair], 32 * B)
                sp.wait_ge(w_in, 128)

            @block.gpsimd
            def _(pool):
                pool.memset(ident[:], 0.0).then_inc(ident_set, 1)
                pool.memset(ones[:], 1.0).then_inc(consts_set, 1)
                pool.memset(power[:], -0.5).then_inc(consts_set, 1)
                pool.wait_ge(ident_set, 1)
                pool.affine_select(out=ident[:], in_=ident[:], compare_op=ALU.not_equal, fill=1.0,
                                   base=0, pattern=[[-1, P]], channel_multiplier=1
                                   ).then_inc(consts_set, 1)
                pool.memset(c_part[:], 0.0).then_inc(zeroed, 1)
                pool.memset(down[:], 0.0).then_inc(zeroed, 1)
                pool.memset(mix[:], 0.0).then_inc(zeroed, 1)
                for n in range(NX):
                    pool.memset(rank[:, n:n + 1], float(NX - n)).then_inc(zeroed, 1)
                pool.wait_ge(zeroed, 3 + NX)
                pool.memset(down[ONE_ROW:ONE_ROW + 1, :], 1.0).then_inc(zeroed, 1)
                pool.wait_ge(zeroed, 4 + NX)
                pool.memset(k_stack[NP3:STACK], SHIFT_UNIT).then_inc(rows_set, 1)
                pool.wait_ge(rows_set, 1)
                pool.wait_ge(consts_set, 3)

                def body(b, last):
                    for t in range(ST):
                        n, k = ST * b + t, t % 2
                        wait(pool, var_ready, n + 1)
                        wait(pool, xn_done, n - 1)
                        pool.tensor_tensor(rstd[:, k:k + 1], var_eps[:, k:k + 1], power[:], ALU.pow
                                           ).then_inc(rstd_done, 1)

                batches(pool, body)

            @block.vector
            def _(dve):
                def low(out, ps, high, n, which):
                    wait(dve, high_done, 2 * n + 1 + which)
                    dve.scalar_tensor_tensor(out=out, in0=ps, scalar=UP, in1=high, op0=ALU.mult,
                                             op1=ALU.subtract).then_inc(low_done, 1)

                def low_q(n, t):
                    k, pair, cols = t % 2, t // 2 % 2, slice(t % 2 * P, (t % 2 + 1) * P)
                    low(q_parts[:, pair, 1, :, cols], q_ps[:, k], q_parts[:, pair, 0, :, cols], n, 0)

                def low_k(n, t):
                    k, pair, cols = t % 2, t // 2 % 2, slice(t % 2 * P, (t % 2 + 1) * P)
                    low(k_parts[:, pair, 1, :, cols], k_ps[:, k, 0:CB], k_parts[:, pair, 0, :, cols], n, 1)

                def variance(n, t, between):
                    k = t % 2
                    dve.wait_ge(x_in[t % ST], 32 * ((n - t % ST) // ST + 1))
                    dve.bn_stats(stats[:, k, 0, :], xin[:, t % ST, 0:512])
                    dve.bn_stats(stats[:, k, 1, :], xin[:, t % ST, 512:1024]).then_inc(stats_done, 1)
                    dve.wait_ge(stats_done, n + 1)
                    between()
                    dve.bn_aggr(mv[:, k, :], stats[:, k]).then_inc(mv_done, 1)

                def centre(n, t):
                    k = t % 2
                    dve.wait_ge(rstd_done, n + 1)
                    wait(dve, turned, n - 1)
                    dve.tensor_scalar(xn[:, k, :], xin[:, t % ST, :], mv[:, k, 0:1], rstd[:, k:k + 1],
                                      ALU.subtract, ALU.mult).then_inc(xn_done, 1)

                def eps(n, t):
                    k = t % 2
                    dve.wait_ge(mv_done, n + 1)
                    wait(dve, rstd_done, n - 1)
                    dve.tensor_scalar_add(var_eps[:, k:k + 1], mv[:, k, 1:2], EPS).then_inc(var_ready, 1)

                nothing = lambda: None

                def body(b, last):
                    for t in range(ST):
                        n = ST * b + t
                        before = not isinstance(n, int) or n > 0
                        more = not (last and t == ST - 1)
                        if more:
                            variance(n + 1, t + 1, lambda: centre(n, t))
                        else:
                            centre(n, t)
                        if before:
                            low_q(n - 1, t + 3)
                        if more:
                            eps(n + 1, t + 1)
                        if before:
                            low_k(n - 1, t + 3)

                variance(0, 0, nothing)
                eps(0, 0)
                batches(dve, body)
                low_q(TILES - 1, ST - 1)
                low_k(TILES - 1, ST - 1)

            @block.tensor
            def _(pe):
                pe.wait_ge(consts_set, 3)

                def body(b, last):
                    for t in range(ST):
                        n, k = ST * b + t, t % 2
                        pe.wait_ge(xn_done, n + 1)
                        wait(pe, low_done, 2 * n - 2)
                        for h in range(KV):
                            pe.transpose(q_ps[:, k, h, :], xn[:, k, h * P:(h + 1) * P], ident[:])
                        for c in range(CB):
                            ins = pe.transpose(k_ps[:, k, c, :], cin[:, t, c * P:(c + 1) * P], ident[:])
                        ins.then_inc(turned, 1)

                batches(pe, body)

            @block.scalar
            def _(act):
                def body(b, last):
                    for t in range(ST):
                        n, k, pair, half = ST * b + t, t % 2, t // 2, t % 2
                        cols = slice(half * P, (half + 1) * P)
                        act.wait_ge(turned, n + 1)
                        if half == 0:
                            wait(act, split_out[pair], 32 * b)
                        act.activation(q_parts[:, pair, 0, :, cols], q_ps[:, k], ACT.Copy, scale=UP
                                       ).then_inc(high_done, 1)
                        act.activation(k_parts[:, pair, 0, :, cols], k_ps[:, k, 0:CB], ACT.Copy, scale=UP
                                       ).then_inc(high_done, 1)

                batches(act, body)

        with ExitStack() as own:
            sb = lambda name, shape, dt: own.enter_context(nc.sbuf_tensor(name, shape, dt))
            row_max = sb("row_max", [P, 2, G * ST], f32)
            shift = sb("shift", [G * ST, 2, 2, P], f16)
            v_in = sb("v_in", [P, 2, ST, D], f32)
            x_res = sb("x_res", [P, 2, ST, P], f32)
            x_att = sb("x_att", [P, 2, ST, P], f32)
            probs = sb("probs", [P, 2, ST, G, S], f32)
            sums = sb("sums", [P, 2, 2, G, S], f32)
            o_raw = sb("o_raw", [P, 2, S], f32)
            den_t = sb("den_t", [P, S], f32)
            inv_t = sb("inv_t", [P, S // D], f32)
            inv = sb("inv", [P, S], f32)
            o_norm = sb("o_norm", [P, S], f32)
            s_ps = own.enter_context(nc.psum_tensor("s_ps", [P, 2, 2, S], f32))
            st_ps = own.enter_context(nc.psum_tensor("st_ps", [P, 2, S], f32))
            o_ps = own.enter_context(nc.psum_tensor("o_ps", [P, S], f32))
            turn_ps = own.enter_context(nc.psum_tensor("turn_ps", [P, S], f32))

            shift_in = [sem("shift_in0"), sem("shift_in1")]
            v_sem = [sem("v_in0"), sem("v_in1")]
            res_in = [sem("res_in0"), sem("res_in1")]
            a_out = [sem("a_out0"), sem("a_out1")]
            max_scored, reduced, max_turned = sem("max_scored"), sem("reduced"), sem("max_turned")
            shift_high, shift_low = sem("shift_high"), sem("shift_low")
            scored, exped, pv_done = sem("scored"), sem("exped"), sem("pv_done")
            front_done, back_done = sem("front_done"), sem("back_done")
            den_done, o_copied, o_turned = sem("den_done"), sem("o_copied"), sem("o_turned")
            den_turned, inv_made, inv_spread = sem("den_turned"), sem("inv_made"), sem("inv_spread")
            o_normed, res_added = sem("o_normed"), sem("res_added")
            total_pool, total_dve = sem("total_pool"), sem("total_dve")
            block = own.enter_context(nc.Block())

            DVE_HEADS = 1
            NMC = G * ST // 2
            NSC = ST * G
            LEAD = 4
            live = lambda u: not isinstance(u, int) or 0 <= u < UNITS

            def steps(eng, body):
                def step(j, k):
                    def at(i):
                        jj, kk = j + (k + i) // SLOTS, (k + i) % SLOTS
                        return (SLOTS * jj + kk, jj // (KV // SLOTS),
                                jj % (KV // SLOTS) * SLOTS + kk)
                    body(SLOTS * j + k, k, at)

                for j in (-1, 0):
                    for k in range(SLOTS):
                        step(j, k)
                with eng.Fori(1, UNITS // SLOTS - 1) as j:
                    for k in range(SLOTS):
                        step(j, k)
                for u in range(UNITS - SLOTS, UNITS + 2):
                    step(u // SLOTS, u % SLOTS)

            @block.gpsimd
            def _(pool):
                def body(u, k, at):
                    if live(u):
                        wait(pool, exped, NSC * (u + 1))
                        wait(pool, den_done, u - 1)
                        pool.tensor_tensor(sums[:, k % 2, 1], probs[:, k % 2, 2], probs[:, k % 2, 3],
                                           ALU.add).then_inc(back_done, 1)
                        wait(pool, back_done, u + 1)
                        pool.tensor_tensor(sums[:, k % 2, 0, DVE_HEADS:], sums[:, k % 2, 0, DVE_HEADS:],
                                           sums[:, k % 2, 1, DVE_HEADS:], ALU.add).then_inc(total_pool, 1)
                    if live(u + 1):
                        s = (k + 1) % 2
                        wait(pool, exped, NSC * (u + 1) + NSC // 2)
                        wait(pool, den_done, u)
                        pool.tensor_tensor(sums[:, s, 0], probs[:, s, 0], probs[:, s, 1], ALU.add
                                           ).then_inc(front_done, 1)

                steps(pool, body)

            @block.sync
            def _(sp):
                def body(u, k, at):
                    if isinstance(u, int) and u == UNITS - 1:
                        for s in range(2):
                            sp.wait_ge(a_out[s], 16 * (KV // 2))
                        for t in range(ST):
                            sp.dma_start(xa0[:, t, :], x_tiles[t]).then_inc(t_in[t], 16)
                    if live(u + 1):
                        v, b, h = at(1)
                        s = (k + 1) % 2
                        wait(sp, pv_done, ST * (v - 1))
                        sp.dma_start(v_in[:, s], ctx_in[bass.ds(b, 1), :, bass.ds(h * D, D)]
                                     .rearrange("o (t p) d -> p (o t) d", p=P)).then_inc(v_sem[s], 16)
                    if live(u):
                        v, b, h = at(0)
                        wait(sp, res_added, v - 1)
                        sp.dma_start(x_res[:, k % 2], x[bass.ds(b, 1), :, bass.ds(h * P, P)]
                                     .rearrange("o (t p) e -> p (o t) e", p=P)).then_inc(res_in[k % 2], 16)
                    if live(u - 2):
                        v, b, h = at(-2)
                        wait(sp, res_added, v + 1)
                        sp.dma_start(y_scr[bass.ds(b, 1), :, bass.ds(h * P, P)]
                                     .rearrange("o (t p) e -> p (o t) e", p=P), x_att[:, k % 2]
                                     ).then_inc(a_out[k % 2], 16)
                    if live(u + LEAD) and live(u):
                        v, b, h = at(LEAD)
                        wait(sp, scored, NSC * (v - 3))
                        load_stacks(sp, b, h, k)
                    if live(u + 2):
                        v, s = u + 2, k % 2
                        wait(sp, shift_low, v + 1)
                        for part in range(2):
                            sp.dma_start(q_stack[NP3 + part:NP3 + part + 1, (k + 2) % SLOTS]
                                         .rearrange("r g s -> r (g s)"), shift[:, s, part, :]
                                         ).then_inc(shift_in[s], 16)

                steps(sp, body)
                for s in range(2):
                    sp.wait_ge(a_out[s], 16 * (UNITS // 2))

            @block.tensor
            def _(pe):
                pe.wait_ge(rows_set, 1)

                def score_rows(u, k, c):
                    for i in range(2):
                        g, t = (2 * c + i) // ST, (2 * c + i) % ST
                        last = pe.matmul(s_ps[:, c % 2, i, :], q_stack[0:NP3, k, g, t * P:(t + 1) * P],
                                         k_stack[0:NP3, k, :], start=True, stop=True)
                    last.then_inc(max_scored, 1)

                def ffn_weights():
                    pe.wait_ge(reduced, NMC * UNITS)
                    pe.wait_ge(prep, 1)
                    for half in range(2):
                        for i in range(4):
                            last = pe.transpose(s_ps[0:NE, 0, half, i * P:(i + 1) * P],
                                                deg_cols[:, 4 * half + i, :], ident[:])
                        last.then_inc(down_turned, 1)
                    pe.wait_ge(prep, 5)
                    pe.matmul(s_ps[:, 1, 0, 0:WC + 2 * NX], ones[:], c_part[:], start=True, stop=True
                              ).then_inc(folded, 1)

                def body(u, k, at):
                    if isinstance(u, int) and u == UNITS:
                        ffn_weights()
                    k3, k1 = (k + 3) % SLOTS, (k + 1) % SLOTS
                    def score_pair(t, pair):
                        if t == 0 and pair == 0:
                            wait(pe, shift_in[k1 % 2], 32 * (at(1)[0] // 2 + 1))
                        for g in (2 * pair, 2 * pair + 1):
                            n = t * G + g
                            wait(pe, exped, NSC * (u + 1) + n - 1)
                            pe.matmul(st_ps[:, n % 2, :], k_stack[:, k1, t * P:(t + 1) * P],
                                      q_stack[:, k1, g, :], start=True, stop=True).then_inc(scored, 1)

                    for t in range(ST):
                        if live(u + 1):
                            score_pair(t, 0)
                        if live(u + 3):
                            if t == 0:
                                wait(pe, s_in[k3], 96 * (at(3)[0] // SLOTS + 1))
                            for c in (2 * t, 2 * t + 1):
                                wait(pe, reduced, NMC * (u + 3) + c - 1)
                                score_rows(u + 3, k3, c)
                        if t == 0 and live(u - 1):
                            wait(pe, total_pool, u)
                            wait(pe, total_dve, u)
                            wait(pe, res_added, u - 1)
                            for g in range(G):
                                last = pe.matmul(turn_ps[g * D:(g + 1) * D, :], ones[:, 0:D],
                                                 sums[:, (k + 1) % 2, 0, g, :], start=True, stop=True)
                            last.then_inc(den_done, 1)
                        if live(u + 1):
                            score_pair(t, 1)
                        if live(u):
                            s = k % 2
                            if t == 0:
                                wait(pe, v_sem[s], 16 * (at(0)[0] // 2 + 1))
                                wait(pe, o_copied, u)
                                wait(pe, exped, NSC * (u + 1))
                            for g in range(G):
                                last = pe.matmul(o_ps[g * D:(g + 1) * D, :], v_in[:, s, t, :],
                                                 probs[:, s, t, g, :], start=(t == 0), stop=(t == ST - 1))
                            last.then_inc(pv_done, 1)
                        if t == 1 and live(u + 2):
                            wait(pe, reduced, NMC * (u + 3))
                            wait(pe, den_turned, u)
                            pe.transpose(turn_ps[0:G * ST, 0:P], row_max[:, k % 2, :], ident[:]
                                         ).then_inc(max_turned, 1)
                        if t == 2 and live(u - 1):
                            wait(pe, o_normed, u)
                            wait(pe, shift_low, min(u + 3, UNITS) if isinstance(u, int) else u + 3)
                            for i in range(ST):
                                last = pe.transpose(turn_ps[:, i * P:(i + 1) * P],
                                                    o_norm[:, i * P:(i + 1) * P], ident[:])
                            last.then_inc(o_turned, 1)

                steps(pe, body)

            @block.scalar
            def _(act):
                def ffn_weights():
                    for half in range(2):
                        act.wait_ge(down_turned, half + 1)
                        act.activation(down[0:NE, :].rearrange("m (p c) -> m c p", c=EC)[:, 4 * half:4 * half + 4, :],
                                       s_ps[0:NE, 0, half].rearrange("m (c p) -> m c p", p=P), ACT.Copy
                                       ).then_inc(down_copied, 1)
                    act.wait_ge(folded, 1)
                    act.activation(cst[:], s_ps[:, 1, 0, 0:WC + 2 * NX], ACT.Copy).then_inc(cst_done, 1)
                    act.wait_ge(cst_done, 1)
                    act.activation(neg_slope[:], cst[:, WC + NX:], ACT.Copy, scale=-1.0).then_inc(cst_done, 1)

                def body(u, k, at):
                    if live(u - 1):
                        wait(act, pv_done, ST * u)
                        wait(act, o_normed, u - 2)
                        act.activation(o_raw[:, (k + 1) % 2, :], o_ps[:], ACT.Copy).then_inc(o_copied, 1)
                    for t in range(ST):
                        if live(u + 1):
                            s = (k + 1) % 2
                            wait(act, pv_done, ST * (u - 1) + t + 1)
                            wait(act, front_done if t < ST // 2 else back_done, u)
                            for g in range(G):
                                n = t * G + g
                                wait(act, scored, NSC * (u + 1) + n + 1)
                                act.activation(probs[:, s, t, g, :], st_ps[:, n % 2, :], ACT.Exp,
                                               scale=EXP_SCALE).then_inc(exped, 1)
                        if t == 1 and live(u + 2):
                            wait(act, max_turned, u + 3)
                            wait(act, shift_in[k % 2], 32 * (at(2)[0] // 2))
                            act.activation(shift[:, k % 2, 0, :], turn_ps[0:G * ST, 0:P], ACT.Copy,
                                           scale=-1.0 / SHIFT_UNIT).then_inc(shift_high, 1)
                    if isinstance(u, int) and u == UNITS:
                        ffn_weights()

                steps(act, body)

            @block.vector
            def _(dve):
                def ffn_weights():
                    dve.wait_ge(w_in, 128)
                    dve.wait_ge(zeroed, 4 + NX)
                    for n, w in enumerate((sel_sb, upd_sb)):
                        dve.tensor_copy(w_all[:, :, n * NE:(n + 1) * NE].rearrange("p c (n s) -> p c n s", n=NX),
                                        w[:].rearrange("p n c s -> p c n s"))
                    dve.tensor_copy(deg_cols[:].rearrange("p c (n s) -> p c n s", n=NX),
                                    deg_sb[:].rearrange("p n c s -> p c n s"))
                    dve.tensor_scalar(w_all[:, :, 2 * NE:], mu_sb[:].rearrange("p n c -> p c n"), -2.0, None,
                                      ALU.mult).then_inc(prep, 1)
                    for n, (w, m) in enumerate(((sel_sb, mu_sb), (upd_sb, deb_sb))):
                        dve.tensor_tensor(prod[:, n], w[:].rearrange("p n c s -> p n s c"),
                                          m[:].unsqueeze(2).to_broadcast([P, NX, NS, EC]), ALU.mult)
                    dve.scalar_tensor_tensor(out=prod[:, 2, :, 0, :], in0=mu_sb[:], scalar=-1.0, in1=mu_sb[:],
                                             op0=ALU.mult, op1=ALU.mult).then_inc(prep, 1)
                    dve.wait_ge(prep, 2)
                    for n in range(2):
                        dve.reduce_sum(c_part[:, n * NE:(n + 1) * NE],
                                       prod[:, n].rearrange("p n s c -> p (n s) c"), AX.X).then_inc(prep, 1)
                    dve.reduce_sum(c_part[:, 2 * NE:WC], prod[:, 2, :, 0, :], AX.X).then_inc(prep, 1)

                def body(u, k, at):
                    if isinstance(u, int) and u == UNITS - 1:
                        ffn_weights()
                    s = (k + 1) % 2
                    for c in range(NMC):
                        if live(u + 3):
                            if c == 0:
                                wait(dve, max_turned, u + 2)
                            wait(dve, max_scored, NMC * (u + 3) + c + 1)
                            dve.reduce_max(row_max[:, s, 2 * c:2 * c + 2], s_ps[:, c % 2], AX.X
                                           ).then_inc(reduced, 1)
                        if live(u - 1):
                            if c == 1:
                                wait(dve, den_done, u)
                                dve.transpose(den_t[:], turn_ps[:]).then_inc(den_turned, 1)
                                wait(dve, den_turned, u)
                                dve.reciprocal(inv_t[:], den_t[:, 0:S:D]).then_inc(inv_made, 1)
                                wait(dve, inv_made, u)
                                dve.transpose(inv[:].rearrange("p (a b) -> p a b", b=D),
                                              inv_t[:].unsqueeze(2).to_broadcast([P, S // D, D])
                                              ).then_inc(inv_spread, 1)
                            if c == 3:
                                wait(dve, inv_spread, u)
                                wait(dve, o_copied, u)
                                wait(dve, o_turned, u - 1)
                                dve.tensor_tensor(o_norm[:], o_raw[:, s, :], inv[:], ALU.mult
                                                  ).then_inc(o_normed, 1)
                        if c == 3 and live(u + 2):
                            wait(dve, shift_high, u + 3)
                            dve.scalar_tensor_tensor(out=shift[:, k % 2, 1, :], in0=turn_ps[0:G * ST, 0:P],
                                                     scalar=-1.0 / SHIFT_UNIT, in1=shift[:, k % 2, 0, :],
                                                     op0=ALU.mult, op1=ALU.subtract).then_inc(shift_low, 1)
                        if c == 7 and live(u):
                            wait(dve, back_done, u + 1)
                            dve.tensor_tensor(sums[:, k % 2, 0, 0:DVE_HEADS], sums[:, k % 2, 0, 0:DVE_HEADS],
                                              sums[:, k % 2, 1, 0:DVE_HEADS], ALU.add).then_inc(total_dve, 1)
                        if c == 5 and live(u - 1):
                            wait(dve, o_turned, u)
                            wait(dve, res_in[s], 16 * (at(-1)[0] // 2 + 1))
                            wait(dve, a_out[s], 16 * (at(-1)[0] // 2))
                            dve.tensor_tensor(x_att[:, s].rearrange("p t e -> p (t e)"),
                                              x_res[:, s].rearrange("p t e -> p (t e)"), turn_ps[:],
                                              ALU.add).then_inc(res_added, 1)

                steps(dve, body)

        with ExitStack() as own:
            sb = lambda name, shape, dt: own.enter_context(nc.sbuf_tensor(name, shape, dt))
            xa = [xa0] + [sb(f"xa{i}", [P, ST, E], f32) for i in range(1, GROUPS)]
            y = sb("y", [P, 2, E], f32)
            yT = sb("yT", [P, 2, EC, P], f32)
            x_out = sb("x_out", [P, ST, E], f32)
            mixT = sb("mixT", [P, ST, P], f32)
            stats = sb("stats3", [P, 2, 2, 6], f32)
            mv = sb("mv3", [P, GROUPS, ST, 2], f32)
            var_eps = sb("var_eps3", [P, 2], f32)
            neg_mean = sb("neg_mean", [P, 2], f32)
            rstd = sb("rstd3", [P, GROUPS, ST], f32)
            neg_mr = sb("neg_mr", [P, GROUPS, ST], f32)
            z_sb = sb("z_sb", [P, ST, WC], f32)
            sq = sb("sq", [P, ST, NE], f32)
            rows = sb("rows", [P, 12, ST, NX], f32)
            y_sq = sb("y_sq", [P, 2, ST], f32)
            top = sb("top", [P, 2, ST], f32)
            z_e = sb("z_e", [P, ST, NX], f32)
            x_scale = sb("x_scale", [P, GROUPS, ST], f32)
            skip_part = sb("skip_part", [P, ST], f32)
            y_ps = own.enter_context(nc.psum_tensor("y_ps", [P, 2, EC, P], f32))
            z_ps = own.enter_context(nc.psum_tensor("z_ps", [P, 2, 256], f32))
            mix_ps = own.enter_context(nc.psum_tensor("mix_ps", [P, ST, P], f32))
            r_ps = own.enter_context(nc.psum_tensor("r_ps", [P, E], f32))

            t_out = [sem(f"t_out{i}") for i in range(ST)]
            ln_chain, gate_chain = sem("ln_chain"), sem("gate_chain")
            var_ready, rstd_done, y_done = sem("var_ready3"), sem("rstd_done3"), sem("y_done")
            y_turned, yT_done, z_done = sem("y_turned"), sem("yT_done"), sem("z_done")
            z_read, e_ready, e_done, mix_done = sem("z_read"), sem("e_ready"), sem("e_done"), sem("mix_done")
            mix_turned, mixT_done, r_done, final = sem("mix_turned"), sem("mixT_done"), sem("r_done"), sem("final")
            block = own.enter_context(nc.Block())

            def steps(eng, body):
                body(0, 0, True, False)
                body(1, 1, True, True)
                with eng.Fori(0, (B - 3) // GROUPS) as j:
                    for i in range(2, GROUPS + 2):
                        body(GROUPS * j + i, i % GROUPS, True, True)
                for q in range(2 + (B - 3) // GROUPS * GROUPS, B + 1):
                    body(q, q % GROUPS, q < B, True)

            o_tiles = out.rearrange("b (t p) e -> (b t) p e", p=P)

            @block.sync
            def _(sp):
                def load(q, k, t):
                    sp.dma_start(xa[k][:, t, :], x_tiles[bass.ds(ST * q + t, 1)].rearrange("o p e -> (o p) e")
                                 ).then_inc(t_in[ST * k + t], 16)


                def store(q, t):
                    n = ST * q + t
                    sp.wait_ge(final, n + 1)
                    sp.dma_start(o_tiles[bass.ds(n, 1)].rearrange("o p e -> (o p) e"),
                                 x_out[:, t, :]).then_inc(t_out[t], 16)

                def body(q, k, more, before):
                    following = more and not (isinstance(q, int) and q == B - 1)
                    if following:
                        for t in range(ST - 1):
                            load(q + 1, (k + 1) % GROUPS, t)
                    if before and not (isinstance(q, int) and q == 1):
                        store(q - 2, ST - 1)
                    if following:
                        load(q + 1, (k + 1) % GROUPS, ST - 1)
                    if before:
                        for t in range(ST - 1):
                            store(q - 1, t)

                steps(sp, body)
                store(B - 1, ST - 1)
                for t in range(ST):
                    sp.wait_ge(t_out[t], 16 * B)

            @block.gpsimd
            def _(pool):
                def body(q, k, more, before):
                    for t in range(ST):
                        if more:
                            n = ST * q + t
                            wait(pool, var_ready, n + 1)
                            pool.tensor_tensor(rstd[:, k, t:t + 1], var_eps[:, t % 2:t % 2 + 1], power[:],
                                               ALU.pow).then_inc(rstd_done, 1)
                            wait(pool, rstd_done, 2 * n + 1)
                            pool.tensor_tensor(neg_mr[:, k, t:t + 1], rstd[:, k, t:t + 1],
                                               neg_mean[:, t % 2:t % 2 + 1], ALU.mult).then_inc(rstd_done, 1)

                steps(pool, body)

            @block.tensor
            def _(pe):
                def turn(q, t):
                    n = ST * q + t
                    wait(pe, y_done, n + 1)
                    wait(pe, yT_done, n - 1)
                    for c in range(EC):
                        last = pe.transpose(y_ps[:, t % 2, c, :], y[:, t % 2, c:E:EC], ident[:])
                    last.then_inc(y_turned, 1)

                def project(q, t):
                    n = ST * q + t
                    wait(pe, yT_done, n + 1)
                    if t % 2 == 0:
                        wait(pe, z_read, ST // 2 * q + t // 2)
                    for c in range(EC):
                        last = pe.matmul(z_ps[:, t % 2, 0:WC], yT[:, t % 2, c, :], w_all[:, c, :],
                                         start=(c == 0), stop=(c == EC - 1))
                    last.then_inc(z_done, 1)

                def turn_mix(q):
                    wait(pe, mix_done, q + 1)
                    wait(pe, mixT_done, q)
                    for t in range(ST):
                        last = pe.transpose(mix_ps[:, t, :], mix[:, t, :], ident[:])
                    last.then_inc(mix_turned, 1)

                def result(q, t):
                    n = ST * q + t
                    wait(pe, mixT_done, q + 1)
                    wait(pe, final, n)
                    for half in range(2):
                        last = pe.matmul(r_ps[:, half * 512:(half + 1) * 512], mixT[:, t, :],
                                         down[:, half * 512:(half + 1) * 512], start=True, stop=True)
                    last.then_inc(r_done, 1)

                def body(q, k, more, before):
                    following = more and not (isinstance(q, int) and q == B - 1)
                    if not before:
                        turn(q, 0)
                        turn(q, 1)
                        project(q, 0)
                        turn(q, 2)
                        project(q, 1)
                    if before:
                        turn_mix(q - 1)
                        result(q - 1, 0)
                    if more:
                        turn(q, 3)
                        project(q, 2)
                    if before:
                        result(q - 1, 1)
                    if following:
                        turn(q + 1, 0)
                    if more:
                        project(q, 3)
                    if before:
                        result(q - 1, 2)
                    if following:
                        turn(q + 1, 1)
                        project(q + 1, 0)
                    if before:
                        result(q - 1, 3)
                    if following:
                        turn(q + 1, 2)
                        project(q + 1, 1)

                steps(pe, body)

            @block.scalar
            def _(act):
                def normalise(q, k, t):
                    n = ST * q + t
                    wait(act, rstd_done, 2 * n + 2)
                    wait(act, y_turned, n - 1)
                    act.activation(y[:, t % 2, :], xa[k][:, t, :], ACT.Identity, scale=rstd[:, k, t:t + 1],
                                   bias=neg_mr[:, k, t:t + 1]).then_inc(y_done, 1)

                def copy_yT(q, t):
                    n = ST * q + t
                    wait(act, y_turned, n + 1)
                    wait(act, z_done, n - 1)
                    act.activation(yT[:, t % 2], y_ps[:, t % 2], ACT.Copy).then_inc(yT_done, 1)

                def body(q, k, more, before):
                    following = more and not (isinstance(q, int) and q == B - 1)
                    after = (k + 1) % GROUPS
                    if not before:
                        normalise(q, k, 0)
                        normalise(q, k, 1)
                        copy_yT(q, 0)
                        normalise(q, k, 2)
                        copy_yT(q, 1)
                        normalise(q, k, 3)
                        copy_yT(q, 2)
                    if before:
                        wait(act, mix_turned, q)
                        act.activation(mixT[:], mix_ps[:], ACT.Copy).then_inc(mixT_done, 1)
                    if following:
                        normalise(q + 1, after, 0)
                    if more:
                        copy_yT(q, 3)
                    if following:
                        normalise(q + 1, after, 1)
                        copy_yT(q + 1, 0)
                        normalise(q + 1, after, 2)
                    if more:
                        wait(act, e_ready, q + 1)
                        act.activation(z_e[:], rows[:, 7], ACT.Exp).then_inc(e_done, 1)
                    if following:
                        copy_yT(q + 1, 1)
                        normalise(q + 1, after, 3)
                        copy_yT(q + 1, 2)

                steps(act, body)

            @block.vector
            def _(dve):
                LN = 2
                ARGS, GATE = 7, 15

                def moments(q, k, t):
                    n, s = ST * q + t, t % 2
                    wait(dve, t_in[ST * k + t], 16 * ((q - k) // GROUPS + 1))
                    dve.bn_stats(stats[:, s, 0, :], xa[k][:, t, 0:512])
                    dve.bn_stats(stats[:, s, 1, :], xa[k][:, t, 512:1024]).then_inc(ln_chain, 1)
                    dve.wait_ge(ln_chain, LN * n + 1)
                    dve.bn_aggr(mv[:, k, t, :], stats[:, s]).then_inc(ln_chain, 1)
                    dve.wait_ge(ln_chain, LN * n + 2)
                    wait(dve, rstd_done, 2 * n - 2)
                    dve.tensor_scalar(neg_mean[:, s:s + 1], mv[:, k, t, 0:1], -1.0, None, ALU.mult)
                    dve.tensor_scalar_add(var_eps[:, s:s + 1], mv[:, k, t, 1:2], EPS).then_inc(var_ready, 1)

                def read_z(q, pair):
                    n = ST * q + 2 * pair
                    wait(dve, mix_done, q)
                    wait(dve, z_done, n + 2)
                    dve.tensor_tensor(z_sb[:, 2 * pair:2 * pair + 2, :], z_ps[:, :, 0:WC],
                                      cst[:, 0:WC].unsqueeze(1).to_broadcast([P, 2, WC]), ALU.subtract
                                      ).then_inc(z_read, 1)

                row = lambda j: rows[:, j]
                over = lambda v: v.unsqueeze(1).to_broadcast([P, ST, NX])
                each = lambda v: v.unsqueeze(2).to_broadcast([P, ST, NX])

                def linker(q, done):
                    count = [done]

                    def link(ins):
                        count[0] += 1
                        ins.then_inc(gate_chain, 1)
                        dve.wait_ge(gate_chain, GATE * q + count[0])
                    return link, count

                def scores(q, k):
                    link, count = linker(q, 0)
                    dve.wait_ge(z_read, ST // 2 * (q + 1))
                    dve.tensor_tensor(sq[:], z_sb[:, :, 0:NE], z_sb[:, :, 0:NE], ALU.mult)
                    dve.wait_ge(rstd_done, 2 * ST * (q + 1))
                    link(dve.tensor_tensor(y_sq[:, 0, :], mv[:, k, :, 1], rstd[:, k, :], ALU.mult))
                    link(dve.scalar_tensor_tensor(out=y_sq[:, 1, :], in0=y_sq[:, 0, :], scalar=float(E),
                                                  in1=rstd[:, k, :], op0=ALU.mult, op1=ALU.mult))
                    link(dve.tensor_tensor(row(1), z_sb[:, :, 2 * NE:], each(y_sq[:, 1, :]), ALU.add))
                    dve.reduce_sum(row(2).rearrange("p t n -> p (t n)"),
                                   sq[:].rearrange("p t (n s) -> p (t n) s", n=NX), AX.X)
                    link(dve.reciprocal(row(3), row(1)))
                    link(dve.tensor_tensor(row(4), row(2), row(3), ALU.mult))
                    link(dve.tensor_tensor(row(5), row(4), over(cst[:, WC:WC + NX]), ALU.subtract))
                    link(dve.tensor_tensor(row(6), row(5), over(neg_slope[:]), ALU.mult))
                    dve.tensor_scalar_min(row(7), row(6), 87.0).then_inc(e_ready, 1)
                    assert count[0] == ARGS, count

                def gates(q, k):
                    link, count = linker(q, ARGS)
                    dve.wait_ge(e_done, q + 1)
                    link(dve.tensor_scalar_add(row(8), z_e[:], 1.0))
                    link(dve.reciprocal(row(9), row(8)))
                    link(dve.reduce_max(top[:, 0, :], row(9), AX.X))
                    link(dve.tensor_tensor(row(10), row(9), each(top[:, 0, :]), ALU.is_ge))
                    link(dve.tensor_tensor(row(11), row(10), over(rank[:]), ALU.mult))
                    dve.tensor_scalar(skip_part[:], top[:, 0, :], -1.0, 1.0, ALU.mult, ALU.add)
                    link(dve.reduce_max(top[:, 1, :], row(11), AX.X))
                    link(dve.tensor_tensor(row(0), row(11), each(top[:, 1, :]), ALU.is_equal))
                    dve.tensor_tensor(x_scale[:, k, :], skip_part[:], rstd[:, k, :], ALU.mult)
                    wait(dve, mix_turned, q)
                    link(dve.tensor_tensor(mix[:, :, NE:NE + NX], row(0), each(top[:, 0, :]), ALU.mult))
                    dve.tensor_tensor(mix[:, :, ONE_ROW], skip_part[:], neg_mr[:, k, :], ALU.mult)
                    dve.tensor_scalar_add(x_scale[:, k, :], x_scale[:, k, :], 1.0)
                    dve.tensor_tensor(mix[:, :, 0:NE].rearrange("p t (n s) -> p t n s", n=NX),
                                      z_sb[:, :, NE:2 * NE].rearrange("p t (n s) -> p t n s", n=NX),
                                      mix[:, :, NE:NE + NX].unsqueeze(3).to_broadcast([P, ST, NX, NS]),
                                      ALU.mult).then_inc(mix_done, 1)
                    assert count[0] == GATE, count

                def finish(q, k, t):
                    n = ST * q + t
                    wait(dve, r_done, n + 1)
                    wait(dve, t_out[t], 16 * q)
                    dve.scalar_tensor_tensor(out=x_out[:, t, :], in0=xa[k][:, t, :],
                                             scalar=x_scale[:, k, t:t + 1], in1=r_ps[:], op0=ALU.mult,
                                             op1=ALU.add).then_inc(final, 1)

                def body(q, k, more, before):
                    following = more and not (isinstance(q, int) and q == B - 1)
                    after, last = (k + 1) % GROUPS, (k - 1) % GROUPS
                    if not before:
                        for t in range(ST):
                            moments(q, k, t)
                    if following:
                        moments(q + 1, after, 0)
                    if more:
                        read_z(q, 0)
                    if following:
                        moments(q + 1, after, 1)
                    if before:
                        finish(q - 1, last, 0)
                    if following:
                        moments(q + 1, after, 2)
                    if before:
                        finish(q - 1, last, 1)
                    if following:
                        moments(q + 1, after, 3)
                    if more:
                        read_z(q, 1)
                        scores(q, k)
                    if before:
                        finish(q - 1, last, 2)
                    if more:
                        gates(q, k)
                    if before:
                        finish(q - 1, last, 3)

                steps(dve, body)


_INS = ['x', 'ctx_512', 'L0_ffn_select_weight', 'L0_ffn_select_mean_diff', 'L0_ffn_imp_center',
        'L0_ffn_imp_slope', 'L0_ffn_lora_update', 'L0_ffn_lora_degen', 'L0_ffn_bias_w',
        'L0_ffn_debias_w']


def kernel(**inputs):
    import numpy as _np
    import concourse.bacc as _bacc
    from concourse import mybir as _mybir
    from concourse.bass_utils import run_bass_kernel_spmd as _run

    nc = _bacc.Bacc("TRN2", target_bir_lowering=False, num_devices=1)
    arrays, args = {}, []
    for name in _INS:
        a = _np.ascontiguousarray(inputs[name])
        arrays[f"in_{name}_dram"] = a
        args.append(nc.dram_tensor(f"in_{name}_dram", a.shape, _mybir.dt.from_np(a.dtype), kind="ExternalInput").ap())
    args.append(nc.dram_tensor("out_0_dram", inputs['x'].shape, _mybir.dt.float32, kind="ExternalOutput").ap())
    xattn_ffn(nc, *args)
    r = _run(nc, [arrays], core_ids=[0])
    return r.results[0]["out_0_dram"]
```
